# Optimizing a Trainium2 kernel written in Bass

```python
import numpy as np
import jax
import jax.numpy as jnp

def _softmax(x, axis=-1):
    return jax.nn.softmax(x, axis=axis)

def _gelu(x):
    return jax.nn.gelu(x, approximate=True)

def _silu(x):
    return jax.nn.silu(x)

def _sigmoid(x):
    return jax.nn.sigmoid(x)

def _layernorm(x, axis=-1, eps=1e-05):
    m = jnp.mean(x, axis=axis, keepdims=True)
    v = jnp.var(x, axis=axis, keepdims=True)
    return (x - m) / jnp.sqrt(v + eps)

def _scatter_add(tgt, idx, src, axis=0):
    return tgt.at[idx].add(src)

def _segment_sum(src, seg, n):
    return jax.ops.segment_sum(src, seg, n)
kernel_name = 'mk_gnn_preln_d2_gnn_r8_374543'

def setup_inputs(seed: int=0):
    np.random.seed(seed)
    _w = jnp.asarray

    def _rec_inputs():
        import jax
        import jax.numpy as jnp
        _gk = jax.random.key(seed)
        x = -0.0003713 + 1 * jax.random.normal(jax.random.fold_in(_gk, 1), (6250, 128), jnp.float32)
        src = jax.random.randint(jax.random.fold_in(_gk, 2), (200000,), 0, 6250, jnp.int32)
        dst = jnp.minimum((6250 * jax.random.uniform(jax.random.fold_in(_gk, 3), (200000,)) ** 2.0).astype(jnp.int32), 49999)
        _o = jnp.argsort(dst, stable=True)
        src = src[_o]
        dst = dst[_o]
        edge_attr_32 = 0.000196303 + 1.00016 * jax.random.normal(jax.random.fold_in(_gk, 11), (200000, 32), jnp.float32)
        return (x, src, dst, edge_attr_32)
    x, src, dst, edge_attr_32 = _rec_inputs()

    def _L0_gnn_setup():
        import jax, jax.numpy as jnp
        import numpy as np
        N_NODES = 12500

        def gcn_conv(x, edge_index, W, b):
            n = x.shape[0]
            h = x @ W
            loop = jnp.arange(n, dtype=edge_index.dtype)
            src = jnp.concatenate([edge_index[0], loop])
            dst = jnp.concatenate([edge_index[1], loop])
            deg = jax.ops.segment_sum(jnp.ones_like(dst, dtype=h.dtype), dst, num_segments=n)
            dinv = jnp.where(deg > 0, jax.lax.rsqrt(deg), 0.0)
            norm = dinv[src] * dinv[dst]
            msg = h[src] * norm[:, None]
            out = jax.ops.segment_sum(msg, dst, num_segments=n)
            return out + b
        key = jax.random.key(seed)
        k1, k2, k3, k4 = jax.random.split(key, 4)
        nfeat = nhid = 128
        x = jax.random.normal(k1, (N_NODES, nfeat), dtype=jnp.float32)
        edge_index = jax.random.randint(k2, (2, 80000), 0, N_NODES, dtype=jnp.int64)
        s = 1.0 / np.sqrt(nfeat)
        W1 = jax.random.normal(k3, (nfeat, nhid), dtype=jnp.float32) * s
        W2 = jax.random.normal(k4, (nhid, nhid), dtype=jnp.float32) * s
        b1 = jnp.zeros((nhid,), dtype=jnp.float32)
        b2 = jnp.zeros((nhid,), dtype=jnp.float32)
        return {'x': x, 'edge_index': edge_index, 'W1': W1, 'b1': b1, 'W2': W2, 'b2': b2}
    _L0_gnn_all = _L0_gnn_setup()
    _L0_gnn_in = {k: v for k, v in _L0_gnn_all.items() if k in ('W1', 'b1', 'W2', 'b2')}
    del _L0_gnn_all

    def _L1_gnn_setup():
        import jax, jax.numpy as jnp
        import numpy as np
        N_NODES = 6250
        N_EDGES = 100000
        NODE_DIM = 128
        EDGE_DIM = 32
        GNN_DIM = 128
        key = jax.random.key(seed)
        k1, k2, k3, k4, k5, k6, k7 = jax.random.split(key, 7)
        x = jax.random.normal(k1, (N_NODES, NODE_DIM), dtype=jnp.float32)
        edge_ids = jax.random.randint(k2, (2, N_EDGES), 0, N_NODES, dtype=jnp.int64)
        edge_attr = jax.random.normal(k3, (N_EDGES, EDGE_DIM), dtype=jnp.float32)
        s1 = 1.0 / np.sqrt(NODE_DIM + EDGE_DIM)
        s2 = 1.0 / np.sqrt(NODE_DIM + GNN_DIM)
        W1 = jax.random.uniform(k4, (NODE_DIM + EDGE_DIM, GNN_DIM), jnp.float32, -s1, s1)
        b1 = jax.random.uniform(k5, (GNN_DIM,), jnp.float32, -s1, s1)
        W2 = jax.random.uniform(k6, (NODE_DIM + GNN_DIM, GNN_DIM), jnp.float32, -s2, s2)
        b2 = jax.random.uniform(k7, (GNN_DIM,), jnp.float32, -s2, s2)
        return {'x': x, 'edge_ids': edge_ids, 'edge_attr': edge_attr, 'W1': W1, 'b1': b1, 'W2': W2, 'b2': b2}
    _L1_gnn_all = _L1_gnn_setup()
    _L1_gnn_in = {k: v for k, v in _L1_gnn_all.items() if k in ('W1', 'b1', 'W2', 'b2')}
    del _L1_gnn_all
    return {'x': x, 'src': src, 'dst': dst, 'edge_attr_32': edge_attr_32, 'L0_gnn_W1': _L0_gnn_in['W1'], 'L0_gnn_b1': _L0_gnn_in['b1'], 'L0_gnn_W2': _L0_gnn_in['W2'], 'L0_gnn_b2': _L0_gnn_in['b2'], 'L1_gnn_W1': _L1_gnn_in['W1'], 'L1_gnn_b1': _L1_gnn_in['b1'], 'L1_gnn_W2': _L1_gnn_in['W2'], 'L1_gnn_b2': _L1_gnn_in['b2']}

def reference(x, src, dst, edge_attr_32, L0_gnn_W1, L0_gnn_b1, L0_gnn_W2, L0_gnn_b2, L1_gnn_W1, L1_gnn_b1, L1_gnn_W2, L1_gnn_b2):
    import jax
    import jax.numpy as jnp

    def _L0_gnn_ref(x, edge_index, W1, b1, W2, b2):
        import jax, jax.numpy as jnp
        import numpy as np
        N_NODES = 12500

        def gcn_conv(x, edge_index, W, b):
            n = x.shape[0]
            h = x @ W
            loop = jnp.arange(n, dtype=edge_index.dtype)
            src = jnp.concatenate([edge_index[0], loop])
            dst = jnp.concatenate([edge_index[1], loop])
            deg = jax.ops.segment_sum(jnp.ones_like(dst, dtype=h.dtype), dst, num_segments=n)
            dinv = jnp.where(deg > 0, jax.lax.rsqrt(deg), 0.0)
            norm = dinv[src] * dinv[dst]
            msg = h[src] * norm[:, None]
            out = jax.ops.segment_sum(msg, dst, num_segments=n)
            return out + b
        h = jax.nn.relu(gcn_conv(x, edge_index, W1, b1))
        out = gcn_conv(h, edge_index, W2, b2)
        return out

    def _L1_gnn_ref(x, edge_ids, edge_attr, W1, b1, W2, b2):
        import jax, jax.numpy as jnp
        import numpy as np
        N_NODES = 6250
        N_EDGES = 100000
        NODE_DIM = 128
        EDGE_DIM = 32
        GNN_DIM = 128
        row, col = (edge_ids[0], edge_ids[1])
        msg = jnp.concatenate((x[row], edge_attr), axis=1)
        msg = jax.nn.relu(msg @ W1 + b1)
        n = x.shape[0]
        sums = jax.ops.segment_sum(msg, col, num_segments=n)
        cnt = jax.ops.segment_sum(jnp.ones((msg.shape[0],), msg.dtype), col, num_segments=n)
        agg = sums / jnp.maximum(cnt, 1.0)[:, None]
        out = jnp.concatenate((x, agg), axis=1)
        return jax.nn.relu(out @ W2 + b2)
    edge_index = jnp.stack([src, dst])
    h = jnp.maximum(_layernorm(x, axis=-1), 0.0)
    x = x + _L0_gnn_ref(h, edge_index, L0_gnn_W1, L0_gnn_b1, L0_gnn_W2, L0_gnn_b2)
    h = jnp.maximum(_layernorm(x, axis=-1), 0.0)
    x = x + _L1_gnn_ref(h, edge_index, edge_attr_32, L1_gnn_W1, L1_gnn_b1, L1_gnn_W2, L1_gnn_b2)
    return x

_drawn_inputs = setup_inputs


def setup_inputs(seed=0):
    import zlib

    import numpy as np

    out = dict(_drawn_inputs(seed))
    spreads = {'L0_gnn_b1': (0.0, 0.1), 'L0_gnn_b2': (0.0, 0.1)}
    factors = {'edge_attr_32': 6.444, 'L1_gnn_b1': 8.0}
    for name, (base, spread) in spreads.items():
        noise = np.random.default_rng([zlib.crc32(name.encode()), seed]).standard_normal(out[name].shape)
        drawn = base * np.exp(spread * noise) if base else spread * noise
        out[name] = jnp.asarray(drawn.astype(out[name].dtype))
    for name, factor in factors.items():
        out[name] = (out[name] * factor).astype(out[name].dtype)
    return out
```

```python
from contextlib import ExitStack

import concourse.bass as bass
from concourse import mybir

F32 = mybir.dt.float32
BF16 = mybir.dt.bfloat16
I32 = mybir.dt.int32
ALU = mybir.AluOpType
ACT = mybir.ActivationFunctionType
AX = mybir.AxisListType

P = 128
N = 6250
E = 200000
D = 128
DE = 32
GB = 4
NG = 13
NB = GB * NG
NP = NB * P
GN = GB * P
TC = 4
CE = TC * P
SLOTS = 8
HALF = SLOTS // 2
NCH = 392
NT = NCH * TC
EP = NT * P
TURNS = NCH // SLOTS
CR = 98
CQ = NCH // CR
HT = 8
HSTEPS = NT // (2 * HT)
EPS = 1e-5
assert NP >= N + P and EP >= E and NCH % SLOTS == 0 and NT % (2 * HT) == 0


def build(nc, t, out):
    with ExitStack() as ctx:
        def sb(name, shape, dt=F32):
            return ctx.enter_context(nc.sbuf_tensor(name, shape, dt))

        def ps(name, shape):
            return ctx.enter_context(nc.psum_tensor(name, shape, F32))

        def sem(name):
            return ctx.enter_context(nc.semaphore(name))

        tables = [nc.dram_tensor(f"table{k}", (NP, D), F32, kind="Internal").ap() for k in range(3)]
        windows_dram = nc.dram_tensor("windows", (2, NCH), I32, kind="Internal").ap()

        consts = sb("consts", [P, 2 * P])
        ident, iota = consts[:, 0:P], consts[:, P:2 * P]
        iota_bf = sb("iota_bf", [P, P], BF16)
        ones = sb("ones", [P, P])
        conv_w = sb("conv_w", [P, 2, D])
        conv_b = sb("conv_b", [P, 2])
        msg_w = sb("msg_w", [P, D])
        msg_b = sb("msg_b", [P, D])
        edge_w = sb("edge_w", [P, TC, D])
        upd_w = sb("upd_w", [P, 2, D])
        upd_b = sb("upd_b", [P, D])
        x = sb("x", [P, NB, D])
        agg = sb("agg", [P, NP])
        dinv_row = sb("dinv_row", [P, NP])
        h2 = sb("h2", [P, NP])
        count = sb("count", [P, NB])
        degree = sb("degree", [P, NB])
        dinv = sb("dinv", [P, NB])
        atleast1 = sb("atleast1", [P, NB])
        inv_count = sb("inv_count", [P, NB])
        dst_i = sb("dst_i", [P, NT], I32)
        part_i = sb("part_i", [P, NT], I32)
        dst_lo = sb("dst_lo", [P, NT], BF16)
        dst_hi = sb("dst_hi", [P, NT], BF16)
        dst_rel = sb("dst_rel", [P, NT])
        rows_i = sb("rows_i", [P, CE], I32)
        chunk_min = sb("chunk_min", [P, CQ], I32)
        chunk_max = sb("chunk_max", [P, CQ], I32)
        span = sb("span", [P, CQ], I32)
        extra = sb("extra", [P, CQ], I32)
        window = sb("window", [P, 2, NCH], I32)
        upto = sb("upto", [1, NCH])
        ahead = sb("ahead", [1, NCH], I32)
        idx = sb("idx", [P, 2, HALF * TC], I32)
        rows = sb("rows", [P, SLOTS, TC * D])
        onehot = sb("onehot", [P, 2, TC, P])
        onehot_x = sb("onehot_x", [P, TC, P])
        iota_x = sb("iota_x", [P, P])
        msgs = sb("msgs", [P, 2, TC * D])
        attr = sb("attr", [P, SLOTS, P])
        hot_lo = sb("hot_lo", [P, 2, HT, P], BF16)
        hot_hi = sb("hot_hi", [P, 2, HT, NB], BF16)
        zero_bf = sb("zero_bf", [P, P], BF16)
        stats = sb("stats", [P, GB, 6])
        moments = sb("moments", [P, GB, 2])
        std = sb("std", [P, GB])
        rstd = sb("rstd", [P, GB])
        eps = sb("eps", [P, 1])
        degree_root = sb("degree_root", [P, NB])
        normed = sb("normed", [P, GB, D])
        feat = sb("feat", [P, GN])
        feat_agg = sb("feat_agg", [P, GN])
        scaled = sb("scaled", [P, GN])
        tab = sb("tab", [P, GB, D])
        diag = sb("diag", [P, GB, P])

        ps_sum = [ps("ps_sum0", [P, 512]), ps("ps_sum1", [P, 512])]
        ps_extra = ps("ps_extra", [P, 512])
        ps_pre = [ps("ps_pre0", [P, 512]), ps("ps_pre1", [P, 512])]
        ps_turn = ps("ps_turn", [P, 512])
        ps_node = ps("ps_node", [P, 512])
        ps_feat = ps("ps_feat", [P, 512])

        loaded = sem("loaded")
        rows_loaded = sem("rows_loaded")
        windows_stored = sem("windows_stored")
        windows_loaded = sem("windows_loaded")
        dve_did = sem("dve_did")
        iota_ready = sem("iota_ready")
        parts_ready = sem("parts_ready")
        ready_setup = sem("ready_setup")
        lo_ready = sem("lo_ready")
        hi_ready = sem("hi_ready")
        hist_done = sem("hist_done")
        count_ready = sem("count_ready")
        dinv_ready = sem("dinv_ready")
        diag_ready = sem("diag_ready")
        row_summed = sem("row_summed")
        row_copied = sem("row_copied")
        block_w_ready = sem("block_w_ready")
        ph = [{k: sem(f"{k}_{n}") for k in ("tab_done", "stored", "normed", "turned", "feat", "nodes", "scaled",
                                            "shifted", "turned2", "freed", "agg_done", "tab_free")} for n in range(3)]
        es = [{k: sem(f"{k}_{n}") for k in ("idx_loaded_a", "idx_loaded_b", "granted", "onehot", "summed", "added",
                                            "x_iota", "x_onehot", "x_summed", "x_added")}
              for n in range(3)]
        for n in range(3):
            es[n]["gathered"] = [sem(f"gathered_{n}_{s}") for s in range(SLOTS)]
        attr_loaded = [sem("attr_loaded_a"), sem("attr_loaded_b")]
        pre_ready = sem("pre_ready")
        msgs_ready = sem("msgs_ready")
        count_in_parts = sem("count_in_parts")
        windows_done = sem("windows_done")
        h2_ready = sem("h2_ready")
        ln_steps = [sem(f"ln_steps_{n}") for n in range(3)]
        fin_steps = sem("fin_steps")
        held = sem("held")
        degree_ready = sem("degree_ready")
        root_ready = sem("root_ready")
        moments_ready = [sem(f"moments_ready_{n}") for n in range(3)]
        std_ready = [sem(f"std_ready_{n}") for n in range(3)]
        fin = {k: sem(f"fin_{k}") for k in ("copied", "multiplied", "t", "u", "out", "out_free", "stored")}

        block = ctx.enter_context(nc.Block())
        N_LOADS = 12

        @block.sync
        def _(sp):
            sp.dma_start(dst_i[:], t["dst_t"]).then_inc(loaded, 16)
            sp.dma_start(consts[:], t["consts"]).then_inc(loaded, 16)
            sp.dma_start(x[:], t["x_nodes"]).then_inc(loaded, 16)
            sp.dma_start(conv_w[:, 0], t["L0_gnn_W1"]).then_inc(loaded, 16)
            sp.dma_start(conv_w[:, 1], t["L0_gnn_W2"]).then_inc(loaded, 16)
            sp.dma_start(conv_b[:, 0:1], t["L0_gnn_b1"].rearrange("(p a) -> p a", a=1)).then_inc(loaded, 16)
            sp.dma_start(conv_b[:, 1:2], t["L0_gnn_b2"].rearrange("(p a) -> p a", a=1)).then_inc(loaded, 16)
            sp.dma_start(msg_w[:], t["L1_gnn_W1"][0:D, :]).then_inc(loaded, 16)
            sp.dma_start(msg_b[:], t["L1_gnn_b1"].rearrange("(a d) -> a d", a=1).to_broadcast([P, D])).then_inc(loaded, 16)
            sp.dma_start(upd_w[:, 0], t["L1_gnn_W2"][0:D, :]).then_inc(loaded, 16)
            sp.dma_start(upd_w[:, 1], t["L1_gnn_W2"][D:2 * D, :]).then_inc(loaded, 16)
            sp.dma_start(upd_b[:], t["L1_gnn_b2"].rearrange("(a d) -> a d", a=1).to_broadcast([P, D])).then_inc(loaded, 16)
            sp.wait_ge(ready_setup, 1)
            for j in range(TC):
                sp.dma_start(edge_w[DE * j:DE * (j + 1), j, :], t["L1_gnn_W1"][D:D + DE, :]).then_inc(block_w_ready, 16)
            for q in range(CQ):
                if q:
                    sp.wait_ge(parts_ready, q)
                sp.dma_start(rows_i[0:CR, :], t["dst_rows"][:, q]).then_inc(rows_loaded, 16)
            sp.wait_ge(parts_ready, CQ + 1)
            sp.dma_start(windows_dram[0].rearrange("(p q) -> p q", q=CQ), chunk_min[0:CR, :]).then_inc(windows_stored, 16)
            sp.dma_start(windows_dram[1].rearrange("(p q) -> p q", q=CQ), extra[0:CR, :]).then_inc(windows_stored, 16)
            sp.wait_ge(windows_stored, 32)
            sp.dma_start(window[:], windows_dram.rearrange("(a r) c -> a r c", a=1).to_broadcast([P, 2, NCH])
                         ).then_inc(windows_loaded, 16)

            def store_table(n):
                table = tables[n].rearrange("(g b p) d -> g p b d", b=GB, p=P)
                sp.sem_inc(ph[n]["tab_free"], 1)
                with sp.Fori(0, NG) as g:
                    sp.wait_ge(ph[n]["tab_done"], g + 1)
                    sp.dma_start(table[bass.ds(g, 1)].rearrange("a p b d -> (a p) b d"), tab[:]).then_inc(ph[n]["stored"], 16)
                    sp.wait_ge(ph[n]["stored"], g * 16 + 16)
                    sp.sem_inc(ph[n]["tab_free"], 1)

            def load_edges(n):
                with sp.Fori(0, TURNS) as i:
                    for h in range(2):
                        sp.wait_ge(es[n]["added"], i * SLOTS + HALF * (h + 1))
                        sp.dma_start(idx[:, h], t["src_t"][:, bass.ds(i * (SLOTS * TC) + h * HALF * TC, HALF * TC)]
                                     ).then_inc(es[n]["idx_loaded_" + "ab"[h]], 16)
                        if n == 2:
                            sp.dma_start(attr[:, h * HALF:(h + 1) * HALF],
                                         t["attr_t"][:, bass.ds(i * SLOTS + h * HALF, HALF)]).then_inc(attr_loaded[h], 16)

            for n in range(3):
                store_table(n)
                load_edges(n)

            rows_out = out.rearrange("(g b p) d -> g p b d", b=GB, p=P)
            sp.sem_inc(fin["out_free"], 1)
            with sp.Fori(0, NG) as g:
                sp.wait_ge(fin["out"], g + 1)
                sp.dma_start(rows_out[bass.ds(g, 1)].rearrange("a p b d -> (a p) b d"), normed[:]).then_inc(fin["stored"], 16)
                sp.wait_ge(fin["stored"], g * 16 + 16)
                sp.sem_inc(fin["out_free"], 1)
            sp.wait_ge(fin["stored"], 16 * NG)

        @block.gpsimd
        def _(pool):
            for n in range(3):
                e = es[n]
                pool.wait_ge(ph[n]["stored"], 16 * NG)
                with pool.Fori(0, TURNS) as i:
                    for h in range(2):
                        pool.wait_ge(e["idx_loaded_" + "ab"[h]], i * 16 + 16)
                        pool.sem_inc(e["granted"])
                        for s in range(h * HALF, (h + 1) * HALF):
                            for j in range(TC):
                                k = (s % HALF) * TC + j
                                nc.gpsimd.indirect_dma_start(
                                    rows[:, s, j * D:(j + 1) * D], None, tables[n],
                                    bass.IndirectOffsetOnAxis(ap=idx[:, h, k:k + 1], axis=0),
                                ).then_inc(e["gathered"][s], 16)

        @block.tensor
        def _(pe):
            mm = nc.tensor.matmul
            pe.wait_ge(loaded, 16 * N_LOADS)
            pe.wait_ge(ready_setup, 1)
            mm(ps_node[:, 0:NB], zero_bf[:], zero_bf[:, 0:NB], start=True, stop=False, skip_group_check=True)
            pe.sem_inc(hist_done, 2)
            with pe.Fori(0, HSTEPS) as i:
                for s in range(2):
                    pe.wait_ge(lo_ready, i * 2 + s + 1)
                    pe.wait_ge(hi_ready, i * 2 + s + 1)
                    for j in range(HT):
                        last = mm(ps_node[:, 0:NB], hot_lo[:, s, j], hot_hi[:, s, j], start=False, stop=False,
                                  skip_group_check=True)
                    last.then_inc(hist_done, 1)
            mm(ps_node[:, 0:NB], zero_bf[:], zero_bf[:, 0:NB], start=False, stop=True,
               skip_group_check=True).then_inc(count_ready, 1)
            with pe.Fori(0, NG) as g:
                pe.wait_ge(diag_ready, g + 1)
                pe.wait_ge(row_copied, g + 1)
                mm(ps_feat[:], ones[:], diag[:].rearrange("p b n -> p (b n)"), start=True, stop=True).then_inc(row_summed, 1)

            def turn(dst_ps):
                for b in range(GB):
                    last = nc.tensor.transpose(dst_ps[:, b * P:(b + 1) * P], normed[:, b], ident)
                return last

            def products(n, w, also_feat):
                s = ph[n]
                for b in range(GB):
                    last = mm(ps_node[:, b * D:(b + 1) * D], feat[:, b * P:(b + 1) * P], w, start=True, stop=True)
                if also_feat:
                    last = mm(ps_feat[:], w, feat[:], start=True, stop=True)
                last.then_inc(s["nodes"], 1)

            def windows(n, c, s, lhs, e):
                nx = pe.value_load(window[0:1, 1, bass.ds(c, 1)], min_val=0, max_val=NB)
                with pe.If(nx > 0):
                    a = pe.value_load(ahead[0:1, bass.ds(c, 1)], min_val=0, max_val=NCH * NB)
                    with pe.Fori(0, nx) as k:
                        pe.wait_ge(e["x_onehot"], a + k + 2)
                        pe.wait_ge(e["x_added"], a + k + 1)
                        for j in range(TC):
                            last = mm(ps_extra[:, 0:P], lhs[:, j * D:(j + 1) * D], onehot_x[:, j], start=(j == 0), stop=(j == TC - 1))
                        last.then_inc(e["x_summed"], 1)
                pe.wait_ge(e["added"], c + 7)
                pe.wait_ge(e["onehot"], c + 1)
                for j in range(TC):
                    last = mm(ps_sum[s % 2][:, 0:P], lhs[:, j * D:(j + 1) * D], onehot[:, s % 2, j], start=(j == 0), stop=(j == TC - 1))
                last.then_inc(e["summed"], 1)

            for n in range(3):
                s = ph[n]
                with pe.Fori(0, NG) as g:
                    if n == 2:
                        pe.wait_ge(s["shifted"], g + 1)
                        for b in range(GB):
                            last = nc.tensor.transpose(ps_pre[0][:, b * P:(b + 1) * P], feat_agg[:, b * P:(b + 1) * P], ident)
                        last.then_inc(s["turned2"], 1)
                    if n != 1:
                        pe.wait_ge(s["normed"], g + 1)
                        turn(ps_turn).then_inc(s["turned"], 1)
                    pe.wait_ge(s["feat"], g + 1)
                    pe.wait_ge(s["freed"], g + 1)
                    products(n, conv_w[:, n] if n < 2 else msg_w[:], n < 2)
                e = es[n]
                pe.sem_inc(e["summed"], 2)
                if n == 2:
                    pe.wait_ge(block_w_ready, 16 * TC)
                with pe.Fori(0, TURNS) as i:
                    def before(s):
                        pe.wait_ge(e["gathered"][s], i * (16 * TC) + 16 * TC)
                        if n < 2:
                            return
                        if s % HALF == 0:
                            pe.wait_ge(attr_loaded[s // HALF], i * 16 + 16)
                        pe.wait_ge(msgs_ready, i * SLOTS + s + 1)
                        mm(ps_pre[s % 2][:], attr[:, s], edge_w[:].rearrange("p j d -> p (j d)"), start=True, stop=False)
                        mm(ps_pre[s % 2][:], ident, rows[:, s], start=False, stop=True).then_inc(pre_ready, 1)

                    def after(s):
                        if n == 2:
                            pe.wait_ge(msgs_ready, i * SLOTS + s + 3)
                        windows(n, i * SLOTS + s, s, msgs[:, s % 2] if n == 2 else rows[:, s], e)

                    before(0)
                    for s in range(1, SLOTS):
                        before(s)
                        after(s - 1)
                    after(SLOTS - 1)

            with pe.Fori(0, NG) as g:
                pe.wait_ge(fin["copied"], g * 2 + 2)
                pe.wait_ge(fin["u"], g + 1)
                for b in range(GB):
                    mm(ps_node[:, b * D:(b + 1) * D], feat[:, b * P:(b + 1) * P], upd_w[:, 0], start=True, stop=True)
                for b in range(GB):
                    last = mm(ps_feat[:, b * D:(b + 1) * D], feat_agg[:, b * P:(b + 1) * P], upd_w[:, 1], start=True, stop=True)
                last.then_inc(fin["multiplied"], 1)

        @block.scalar
        def _(act):
            act.wait_ge(degree_ready, 1)
            nc.scalar.activation(degree_root[:], degree[:], ACT.Sqrt).then_inc(root_ready, 1)
            act.sem_inc(row_copied, 1)
            with act.Fori(0, NG) as g:
                act.wait_ge(row_summed, g + 1)
                nc.scalar.activation(dinv_row[:, bass.ds(g * GN, GN)], ps_feat[:], ACT.Copy).then_inc(row_copied, 1)
            for n in range(3):
                s = ph[n]
                with act.Fori(0, NG) as g:
                    if n == 0:
                        act.wait_ge(moments_ready[n], g + 1)
                        nc.scalar.activation(std[:], moments[:, :, 1], ACT.Sqrt, bias=eps[:]).then_inc(std_ready[n], 1)
                        act.wait_ge(s["turned"], g + 1)
                        act.wait_ge(s["freed"], g + 1)
                        nc.scalar.activation(feat[:], ps_turn[:], ACT.Relu).then_inc(s["feat"], 1)
                    elif n == 1:
                        act.wait_ge(s["scaled"], g + 1)
                        act.wait_ge(s["freed"], g + 1)
                        nc.scalar.activation(feat[:], scaled[:], ACT.Relu, bias=conv_b[:, 0:1]).then_inc(s["feat"], 1)
                    else:
                        act.wait_ge(s["scaled"], g + 1)
                        act.wait_ge(s["freed"], g + 1)
                        nc.scalar.activation(feat_agg[:], scaled[:], ACT.Identity, bias=conv_b[:, 1:2]).then_inc(s["shifted"], 1)
                        act.wait_ge(moments_ready[n], g + 1)
                        nc.scalar.activation(std[:], moments[:, :, 1], ACT.Sqrt, bias=eps[:]).then_inc(std_ready[n], 1)
                        act.wait_ge(s["turned"], g + 1)
                        nc.scalar.activation(feat[:], ps_turn[:], ACT.Relu).then_inc(s["feat"], 1)
                        nc.scalar.activation(h2[:, bass.ds(g * GN, GN)], ps_turn[:], ACT.Relu).then_inc(h2_ready, 1)
            e = es[2]
            act.sem_inc(msgs_ready, 2)
            with act.Fori(0, TURNS) as i:
                for s in range(SLOTS):
                    act.wait_ge(pre_ready, i * SLOTS + s + 1)
                    act.wait_ge(e["summed"], i * SLOTS + s + 1)
                    nc.scalar.activation(msgs[:, s % 2], ps_pre[s % 2][:], ACT.Relu).then_inc(msgs_ready, 1)
            act.wait_ge(h2_ready, NG)
            act.wait_ge(e["added"], SLOTS + NCH)
            with act.Fori(0, NG) as g:
                act.wait_ge(fin["t"], g + 1)
                nc.scalar.activation(feat[:], h2[:, bass.ds(g * GN, GN)], ACT.Copy).then_inc(fin["copied"], 1)
                nc.scalar.activation(feat_agg[:], agg[:, bass.ds(g * GN, GN)], ACT.Copy).then_inc(fin["copied"], 1)

        @block.vector
        def _(dve):
            v = nc.vector
            steps = [0]

            def link(ins):
                steps[0] += 1
                ins.then_inc(dve_did, 1)
                dve.wait_ge(dve_did, steps[0])

            def hold(s, value):
                dve.wait_ge(s, value)
                dve.sem_inc(held, 1)

            v.memset(edge_w[:], 0.0).then_inc(dve_did, 1)
            v.memset(ones[:], 1.0).then_inc(dve_did, 1)
            v.memset(zero_bf[:], 0.0).then_inc(dve_did, 1)
            v.memset(eps[:], EPS).then_inc(dve_did, 1)
            steps[0] = 4
            dve.wait_ge(dve_did, 4)
            dve.sem_inc(ready_setup, 1)
            dve.wait_ge(loaded, 16 * N_LOADS)
            link(v.tensor_copy(iota_bf[:], iota))
            link(v.tensor_single_scalar(part_i[:], dst_i[:], P - 1, ALU.bitwise_and))
            link(v.tensor_copy(dst_lo[:], part_i[:]))
            link(v.tensor_single_scalar(part_i[:], dst_i[:], 7, ALU.arith_shift_right))
            v.tensor_copy(dst_hi[:], part_i[:]).then_inc(count_in_parts, 1)
            dve.wait_ge(count_in_parts, 1)
            with dve.Fori(0, HSTEPS) as i:
                for s in range(2):
                    dve.wait_ge(hist_done, i * 2 + s + 1)
                    v.tensor_tensor(hot_lo[:, s], iota_bf[:, None, :].to_broadcast([P, HT, P]),
                                    dst_lo[:, bass.ds(i * (2 * HT) + s * HT, HT)].unsqueeze(2).to_broadcast([P, HT, P]),
                                    ALU.is_equal).then_inc(lo_ready, 1)
                    v.tensor_tensor(hot_hi[:, s], iota_bf[:, None, 0:NB].to_broadcast([P, HT, NB]),
                                    dst_hi[:, bass.ds(i * (2 * HT) + s * HT, HT)].unsqueeze(2).to_broadcast([P, HT, NB]),
                                    ALU.is_equal).then_inc(hi_ready, 1)
            for q in range(CQ):
                dve.wait_ge(rows_loaded, 16 * (q + 1))
                v.tensor_reduce(chunk_min[0:CR, q:q + 1], rows_i[0:CR, :], AX.X, ALU.min).then_inc(dve_did, 1)
                v.tensor_reduce(chunk_max[0:CR, q:q + 1], rows_i[0:CR, :], AX.X, ALU.max).then_inc(dve_did, 1)
                steps[0] += 2
                dve.wait_ge(dve_did, steps[0])
                dve.sem_inc(parts_ready, 1)
            link(v.tensor_tensor(span[0:CR], chunk_max[0:CR], chunk_min[0:CR], ALU.subtract))
            v.tensor_single_scalar(extra[0:CR], span[0:CR], 7, ALU.arith_shift_right).then_inc(parts_ready, 1)
            dve.wait_ge(count_ready, 1)
            link(v.tensor_copy(count[:], ps_node[:, 0:NB]))
            link(v.tensor_scalar(degree[:], count[:], 1.0, None, ALU.add))
            dve.sem_inc(degree_ready, 1)
            dve.wait_ge(root_ready, 1)
            link(v.reciprocal(dinv[:], degree_root[:]))
            link(v.tensor_scalar(atleast1[:], count[:], 1.0, None, ALU.max))
            link(v.reciprocal(inv_count[:], atleast1[:]))
            with dve.Fori(0, NG) as g:
                dve.wait_ge(row_copied, g + 1)
                v.tensor_tensor(diag[:], ident[:, None, :].to_broadcast([P, GB, P]),
                                dinv[:, bass.ds(g * GB, GB)].unsqueeze(2).to_broadcast([P, GB, P]), ALU.mult).then_inc(diag_ready, 1)
            dve.wait_ge(windows_loaded, 16)
            link(v.tensor_tensor(dst_rel[:].rearrange("p (c t) -> p c t", t=TC), dst_i[:].rearrange("p (c t) -> p c t", t=TC),
                                 window[:, 0].unsqueeze(2).to_broadcast([P, NCH, TC]), ALU.subtract))
            link(v.tensor_copy(upto[:], window[0:1, 1, :]))
            link(v.tensor_tensor_scan(upto[:], upto[:], upto[:], 0.0, ALU.add, ALU.bypass))
            v.tensor_tensor(ahead[:], upto[:], window[0:1, 1, :], ALU.subtract).then_inc(windows_done, 1)
            dve.wait_ge(windows_done, 1)
            dve.wait_ge(row_copied, NG + 1)

            def layernorm(src_blocks, n, g):
                s, steps_done = ln_steps[n], g * LN_STEPS
                for b in range(GB):
                    v.bn_stats(stats[:, b], src_blocks(b)).then_inc(s, 1)
                hold(s, steps_done + GB)
                for b in range(GB):
                    last = v.bn_aggr(moments[:, b], stats[:, b])
                last.then_inc(moments_ready[n], 1)
                dve.wait_ge(moments_ready[n], g + 1)
                dve.wait_ge(std_ready[n], g + 1)
                v.reciprocal(rstd[:], std[:]).then_inc(s, 1)
                dve.wait_ge(s, steps_done + GB + 1)
                for b in range(GB):
                    last = v.tensor_scalar(normed[:, b], src_blocks(b), moments[:, b, 0:1], rstd[:, b:b + 1],
                                           ALU.subtract, ALU.mult)
                return last

            LN_STEPS = GB + 1

            def xb(g):
                return lambda b: x[:, bass.ds(g * GB + b, 1)].rearrange("p a d -> p (a d)")

            for n in range(3):
                s = ph[n]
                dve.sem_inc(s["freed"], 1)
                with dve.Fori(0, NG) as g:
                    grp = bass.ds(g * GN, GN)
                    if n == 0:
                        layernorm(xb(g), n, g).then_inc(s["normed"], 1)
                    else:
                        v.tensor_tensor(scaled[:], agg[:, grp], dinv_row[:, grp], ALU.mult).then_inc(s["scaled"], 1)
                    if n == 2:
                        dve.wait_ge(s["turned2"], g + 1)
                        xg = x[:, bass.ds(g * GB, GB)].rearrange("p b d -> p (b d)")
                        v.tensor_tensor(xg, xg, ps_pre[0][:], ALU.add).then_inc(s["agg_done"], 1)
                        hold(s["agg_done"], g + 1)
                        layernorm(xb(g), n, g).then_inc(s["normed"], 1)
                    dve.wait_ge(s["nodes"], g + 1)
                    dve.wait_ge(s["tab_free"], g + 1)
                    nodes = ps_node[:].rearrange("p (b d) -> p b d", b=GB)
                    if n < 2:
                        v.tensor_tensor(tab[:], nodes, dinv[:, bass.ds(g * GB, GB)].unsqueeze(2).to_broadcast([P, GB, D]),
                                        ALU.mult).then_inc(s["tab_done"], 1)
                        v.tensor_tensor(agg[:, grp], ps_feat[:], dinv_row[:, grp], ALU.mult).then_inc(s["agg_done"], 1)
                        dve.wait_ge(s["tab_done"], g + 1)
                        dve.wait_ge(s["agg_done"], g + 1)
                        dve.sem_inc(s["freed"], 1)
                    else:
                        v.tensor_tensor(tab[:], nodes, msg_b[:, None, :].to_broadcast([P, GB, D]), ALU.add).then_inc(s["tab_done"], 1)
                        dve.wait_ge(s["tab_done"], g + 1)
                        dve.sem_inc(s["freed"], 1)
                if n == 2:
                    link(v.memset(agg[:], 0.0))

                e = es[n]
                dve.sem_inc(e["added"], SLOTS)
                dve.sem_inc(e["x_added"], 1)
                dve.sem_inc(e["x_onehot"], 1)
                with dve.Fori(0, TURNS) as i:
                    bases = [None] * SLOTS

                    def hot(s):
                        c = i * SLOTS + s
                        bases[s] = dve.value_load(window[0:1, 0, bass.ds(c, 1)], min_val=0, max_val=NP - P)
                        v.tensor_tensor(onehot[:, s % 2], iota[:, None, :].to_broadcast([P, TC, P]),
                                        dst_rel[:, bass.ds(c * TC, TC)].unsqueeze(2).to_broadcast([P, TC, P]),
                                        ALU.is_equal).then_inc(e["onehot"], 1)

                    def add(s):
                        c = i * SLOTS + s
                        nx = dve.value_load(window[0:1, 1, bass.ds(c, 1)], min_val=0, max_val=NB)
                        with dve.If(nx > 0):
                            a = dve.value_load(ahead[0:1, bass.ds(c, 1)], min_val=0, max_val=NCH * NB)
                            v.tensor_copy(iota_x[:], iota).then_inc(e["x_iota"], 1)
                            dve.drain()
                            with dve.Fori(0, nx) as k:
                                v.tensor_scalar(iota_x[:], iota_x[:], float(P), None, ALU.add).then_inc(e["x_iota"], 1)
                                dve.drain()
                                v.tensor_tensor(onehot_x[:], iota_x[:, None, :].to_broadcast([P, TC, P]),
                                                dst_rel[:, bass.ds(c * TC, TC)].unsqueeze(2).to_broadcast([P, TC, P]),
                                                ALU.is_equal).then_inc(e["x_onehot"], 1)
                                dve.wait_ge(e["x_summed"], a + k + 1)
                                w = agg[:, bass.ds((bases[s] + k * P + P).with_bounds(min_val=0, max_val=NP - P), P)]
                                v.tensor_tensor(w, w, ps_extra[:, 0:P], ALU.add).then_inc(e["x_added"], 1)
                                dve.drain()
                        dve.wait_ge(e["summed"], c + 3)
                        dve.wait_ge(e["added"], c + SLOTS)
                        w = agg[:, bass.ds(bases[s], P)]
                        v.tensor_tensor(w, w, ps_sum[s % 2][:, 0:P], ALU.add).then_inc(e["added"], 1)

                    hot(0)
                    for s in range(1, SLOTS):
                        hot(s)
                        add(s - 1)
                    add(SLOTS - 1)
                dve.wait_ge(e["added"], NCH + SLOTS)

            dve.sem_inc(fin["t"], 1)
            dve.sem_inc(fin["u"], 1)
            nodes = ps_node[:].rearrange("p (b d) -> p b d", b=GB)
            sums = ps_feat[:].rearrange("p (b d) -> p b d", b=GB)
            with dve.Fori(0, NG) as g:
                dve.wait_ge(fin["multiplied"], g + 1)
                v.tensor_tensor(tab[:], sums, inv_count[:, bass.ds(g * GB, GB)].unsqueeze(2).to_broadcast([P, GB, D]),
                                ALU.mult).then_inc(fin_steps, 1)
                dve.wait_ge(fin_steps, g * 4 + 1)
                v.tensor_tensor(tab[:], nodes, tab[:], ALU.add).then_inc(fin_steps, 1)
                dve.wait_ge(fin_steps, g * 4 + 2)
                v.tensor_tensor(tab[:], tab[:], upd_b[:, None, :].to_broadcast([P, GB, D]), ALU.add).then_inc(fin_steps, 1)
                dve.wait_ge(fin_steps, g * 4 + 3)
                v.tensor_scalar(tab[:], tab[:], 0.0, None, ALU.max).then_inc(fin_steps, 1)
                dve.wait_ge(fin_steps, g * 4 + 4)
                dve.sem_inc(fin["t"], 1)
                dve.sem_inc(fin["u"], 1)
                dve.wait_ge(fin["out_free"], g + 1)
                v.tensor_tensor(normed[:], x[:, bass.ds(g * GB, GB)], tab[:], ALU.add).then_inc(fin["out"], 1)
                dve.wait_ge(fin["out"], g + 1)


def kernel(**inputs):
    import numpy as np
    import concourse.bacc as bacc
    from concourse.bass_utils import run_bass_kernel_spmd

    nc = bacc.Bacc("TRN2", target_bir_lowering=False, num_devices=1)
    x = np.zeros((NP, D), np.float32)
    x[:N] = inputs["x"]
    src = np.zeros(EP, np.int32)
    src[:E] = inputs["src"]
    dst = np.full(EP, N, np.int32)
    dst[:E] = inputs["dst"]
    attr = np.zeros((EP, DE), np.float32)
    attr[:E] = inputs["edge_attr_32"]
    arrays = {
        "x_nodes": x.reshape(NB, P, D).transpose(1, 0, 2),
        "src_t": src.reshape(NT, P).T,
        "dst_t": dst.reshape(NT, P).T,
        "dst_rows": dst.reshape(CR, CQ, CE),
        "attr_t": attr.reshape(NCH, TC, P, DE).transpose(1, 3, 0, 2).reshape(P, NCH, P),
        "consts": np.concatenate([np.eye(P, dtype=np.float32), np.tile(np.arange(P, dtype=np.float32), (P, 1))], 1),
    }
    for name in ("L0_gnn_W1", "L0_gnn_b1", "L0_gnn_W2", "L0_gnn_b2", "L1_gnn_W1", "L1_gnn_b1", "L1_gnn_W2", "L1_gnn_b2"):
        arrays[name] = inputs[name]
    arrays = {f"{k}_in": np.ascontiguousarray(a) for k, a in arrays.items()}
    t = {k[:-3]: nc.dram_tensor(k, a.shape, mybir.dt.from_np(a.dtype), kind="ExternalInput").ap() for k, a in arrays.items()}
    out = nc.dram_tensor("out_nodes", (NP, D), F32, kind="ExternalOutput").ap()
    build(nc, t, out)
    r = run_bass_kernel_spmd(nc, [arrays], core_ids=[0])
    return r.results[0]["out_nodes"][:N]
```

```python
from contextlib import ExitStack

import concourse.bass as bass
from concourse import mybir

F32 = mybir.dt.float32
BF16 = mybir.dt.bfloat16
F16 = mybir.dt.float16
I32 = mybir.dt.int32
ALU = mybir.AluOpType
ACT = mybir.ActivationFunctionType
AX = mybir.AxisListType

P = 128
N = 6250
E = 200000
D = 128
DE = 32
GB = 4
NG = 13
NB = GB * NG
NP = NB * P
GN = GB * P
TC = 4
CE = TC * P
SLOTS = 8
HALF = SLOTS // 2
NCH = 392
NT = NCH * TC
EP = NT * P
TURNS = NCH // SLOTS
CR = 98
CQ = NCH // CR
CT = CE * CQ // P
HT = 8
HSTEPS = NT // (2 * HT)
W = 8
STRIP = 256
SW = STRIP // W
STRIPS = 6
DENSE = STRIPS * STRIP
NW = STRIPS * SW
SEG = 8
SEGS = SW // SEG
UNIT = 6
ROW = 16
FIRST_VISITS = (59, 26, 20, 17, 15, 14, 13, 12, 11, 11, 10, 10, 10, 9, 9, 9, 9, 8, 8, 8, 8, 8, 7, 7, 7, 7, 7, 7, 7, 7, 7, 6)
RUNS = (((2, 6), (2, 5)), ((2, 5), (2, 4)), ((4, 4),), ((4, 4),), ((4, 3),))
SB = (N + P - 1) // P
KEYS = W * SB
VISITS = list(FIRST_VISITS) + [k for runs in RUNS for n, k in runs for _ in range(n * SEG)]
VB = (sum(VISITS) + P - 1) // P
EDGE_ROWS = EP // ROW + max(VISITS) * (P // ROW)
PARTS = 3
MASKED = -1048576.0
EXACT = 256.0
EPS = 1e-5
assert NP >= N + P and EP >= E and NCH % SLOTS == 0 and NT % (2 * HT) == 0
assert STRIPS % 2 == 0 and len(VISITS) == NW and KEYS <= 512 and SB == 12 * SEGS + 1 and DENSE % P == 0
assert max(k for runs in RUNS for _, k in runs) <= UNIT


def build(nc, t, out):
    with ExitStack() as ctx:
        def sb(name, shape, dt=F32):
            return ctx.enter_context(nc.sbuf_tensor(name, shape, dt))

        def ps(name, shape):
            return ctx.enter_context(nc.psum_tensor(name, shape, F32))

        def sem(name):
            return ctx.enter_context(nc.semaphore(name))

        tables = [nc.dram_tensor(f"table{k}", (NP, D), F32, kind="Internal").ap() for k in range(3)]
        tiles_dram = nc.dram_tensor("tiles", (2, NT), I32, kind="Internal").ap()
        starts_dram = nc.dram_tensor("starts_of_nodes", (NP, 1), I32, kind="Internal").ap()
        own_dram = nc.dram_tensor("own", (P, NP), F32, kind="Internal").ap()
        counts_dram = nc.dram_tensor("counts", (STRIPS, P, SB * STRIP), BF16, kind="Internal").ap()

        consts = sb("consts", [P, 3 * P + KEYS + VB])
        ident, iota, key_iota = consts[:, 0:P], consts[:, P:2 * P], consts[:, 2 * P:2 * P + KEYS]
        above = consts[:, 2 * P + KEYS:3 * P + KEYS]
        visit_key = consts[:, 3 * P + KEYS:]
        iota_bf = sb("iota_bf", [P, P], BF16)
        ones = sb("ones", [P, P])
        zero_strip = sb("zero_strip", [P, STRIP], BF16)
        conv_w = sb("conv_w", [P, 2, D])
        conv_b = sb("conv_b", [P, 2])
        msg_w = sb("msg_w", [P, D])
        msg_b = sb("msg_b", [P, D])
        edge_w = sb("edge_w", [P, TC, D])
        upd_w = sb("upd_w", [P, 2, D])
        upd_b = sb("upd_b", [P, D])
        agg = sb("agg", [P, NP])
        count = sb("count", [P, NB])
        degree = sb("degree", [P, NB])
        dinv = sb("dinv", [P, NB])
        atleast1 = sb("atleast1", [P, NB])
        inv_count = sb("inv_count", [P, NB])
        region_a = sb("region_a", [P, SB * STRIP])
        region_b = sb("region_b", [P, NB * PARTS * D // 2])
        used = [0]

        def carve(columns, dt=F32):
            a = used[0]
            used[0] += columns
            assert used[0] <= SB * STRIP
            return region_a[:, a:a + columns].bitcast(dt)

        dst_i = carve(NT, I32)
        part_i = carve(NT, I32)
        dst_lo = carve(NT // 2, BF16)
        dst_hi = carve(NT // 2, BF16)
        hot_lo = carve(HT * P, BF16).rearrange("p (s t n) -> p s t n", s=2, t=HT)
        hot_hi = carve(HT * NB, BF16).rearrange("p (s t n) -> p s t n", s=2, t=HT)
        tile_min = carve(NT, I32)
        tile_max = carve(NT, I32)
        rows_i = carve(CE, I32)
        visit_edges = carve(VB * 2 * P, I32).rearrange("p (v k e) -> p v k e", v=VB, k=2)
        part_columns = region_a[:, VB * 2 * P:VB * 3 * P].bitcast(I32)
        assert VB * 3 * P <= 3 * NT + (HT * (P + NB)) 
        split_edges = region_a[:, 0:VB * 2 * P].rearrange("p (v k e) -> p v k e", v=VB, k=2)
        used[0] = 0
        counts = [carve(SB * STRIP // 2, BF16).rearrange("p (h d) -> p h d", h=SB) for _ in range(2)]
        used[0] = 0
        h2 = carve(NP)
        msgs = carve(2 * TC * D).rearrange("p (s d) -> p s d", s=2)
        attr = carve(SLOTS * P).rearrange("p (s d) -> p s d", s=SLOTS)
        parts = region_b[:].bitcast(BF16).rearrange("p (h k d) -> p h k d", h=NB, k=PARTS)
        x1 = region_b[:, 0:NB * D].rearrange("p (b d) -> p b d", d=D)
        dst_rel = sb("dst_rel", [P, NT])
        visit = sb("visit", [P, VB * P, 2])
        visit_now = sb("visit_now", [P, SEG * UNIT, 2])
        visit_plan = sb("visit_plan", [P, 2, VB], I32)
        visit_start = sb("visit_start", [P, VB], I32)
        visit_row = sb("visit_row", [P, VB], I32)
        starts = sb("starts", [P, 3, NB])
        starts_i = sb("starts_i", [NB, P], I32)
        chunk_window = sb("chunk_window", [1, 3, NCH], I32)
        upto = sb("upto", [1, NCH])
        row_min = sb("row_min", [P, CQ * TC], I32)
        row_max = sb("row_max", [P, CQ * TC], I32)
        before_dense = sb("before_dense", [P, 2])
        turns_i = sb("turns_i", [P, 4], I32)
        row_sums = sb("row_sums", [P, NW])
        found = sb("found", [P, 4])
        verdict = sb("verdict", [1, 4])
        flag = sb("flag", [1, 1], I32)
        idx = sb("idx", [P, 2, HALF * TC], I32)
        rows = sb("rows", [P, SLOTS, TC * D])
        onehot = sb("onehot", [P, 2, TC, P])
        onehot_x = sb("onehot_x", [P, TC, P])
        iota_x = sb("iota_x", [P, P])
        iota_key = sb("iota_key", [P, KEYS], F16)
        hot_src = sb("hot_src", [P, 2, UNIT, P], BF16)
        hot_key = sb("hot_key", [P, 2, UNIT, KEYS], BF16)
        zero_bf = sb("zero_bf", [P, P], BF16)
        xg = sb("xg", [P, GB, D])
        stats = sb("stats", [P, GB, 6])
        moments = sb("moments", [P, GB, 2])
        std = sb("std", [P, GB])
        rstd = sb("rstd", [P, GB])
        eps = sb("eps", [P, 1])
        degree_root = sb("degree_root", [P, NB])
        normed = sb("normed", [P, GB, D])
        feat = sb("feat", [P, GN])
        feat_agg = sb("feat_agg", [P, GN])
        scaled = sb("scaled", [P, GN])
        tab = sb("tab", [P, GB, D])
        rest = scaled[:].rearrange("p (b d) -> p b d", b=GB)
        diag = onehot[:, 0]

        ps_sum = [ps("ps_sum0", [P, 512]), ps("ps_sum1", [P, 512])]
        ps_extra = ps("ps_extra", [P, 512])
        ps_pre = [ps("ps_pre0", [P, 512]), ps("ps_pre1", [P, 512])]
        ps_turn = ps("ps_turn", [P, 512])
        ps_node = ps("ps_node", [P, 512])
        ps_feat = ps("ps_feat", [P, 512])

        loaded = sem("loaded")
        setup_ready = sem("setup_ready")
        edge_w_loaded = sem("edge_w_loaded")
        rows_loaded = sem("rows_loaded")
        rows_reduced = sem("rows_reduced")
        tiles_stored = sem("tiles_stored")
        tiles_loaded = sem("tiles_loaded")
        count_copied = sem("count_copied")
        before_ready = sem("before_ready")
        starts_ready = sem("starts_ready")
        starts_turned = sem("starts_turned")
        starts_int = sem("starts_int")
        starts_stored = sem("starts_stored")
        starts_gathered = sem("starts_gathered")
        visit_rows_ready = sem("visit_rows_ready")
        visits_gathered = sem("visits_gathered")
        visits_split = sem("visits_split")
        visits_turned = sem("visits_turned")
        visits_copied = sem("visits_copied")
        tables_ready = sem("tables_ready")
        dve_did = sem("dve_did")
        held = {e: sem(f"held_{e}") for e in ("dve", "act", "pool", "sp")}
        parts_split = sem("parts_split")
        lo_ready = sem("lo_ready")
        hi_ready = sem("hi_ready")
        hist_used = sem("hist_used")
        count_ready = sem("count_ready")
        degree_ready = sem("degree_ready")
        root_ready = sem("root_ready")
        G = {k: sem(f"node_{k}") for k in (
            "stats", "moments", "std", "normed", "turned", "diag", "row", "scaled", "shifted", "back", "x1",
            "feat", "products", "tab", "tab_stored", "tab_free", "own_turned", "own", "part", "rest", "h2", "freed")}
        rstd_ready = sem("rstd_ready")
        x_loaded = sem("x_loaded")
        own_stored = sem("own_stored")
        own_restored = sem("own_restored")
        C = {k: sem(f"count_{k}") for k in ("hot", "built", "evacuated", "stored_a", "stored_b", "loaded_a", "loaded_b")}
        applied = [sem("applied_0"), sem("applied_1")]
        strip_added = [sem("strip_added_0"), sem("strip_added_1")]
        most_ready = sem("most_ready")
        most_turned = sem("most_turned")
        flag_ready = sem("flag_ready")
        full_ready = sem("full_ready")
        dense_done = sem("dense_done")

        def gather_sems(name, every=True, apart=HALF):
            gathered = [sem(f"gathered_{s}_{name}") for s in range(SLOTS // apart)]
            return {"every": every, "apart": apart, "gathered": gathered} | {k: sem(f"{k}_{name}") for k in (
                "idx_a", "idx_b", "onehot", "summed", "added",
                "x_onehot", "x_summed", "x_added")}

        shared_passes = [gather_sems(f"shared_{n}", False, 2) for n in range(2)]
        full_passes = [gather_sems(f"full_{n}") for n in range(2)]
        msg_pass = gather_sems("msg", True, 1)
        attr_loaded = [sem("attr_loaded_a"), sem("attr_loaded_b")]
        pre_ready = sem("pre_ready")
        msgs_ready = sem("msgs_ready")
        fin = {k: sem(f"fin_{k}") for k in ("copied", "multiplied", "free", "out", "out_free", "stored", "steps")}

        block = ctx.enter_context(nc.Block())
        N_LOADS = 12
        LAST = NB // GB

        def group(n, g):
            return g + n * NG

        def turn_at(first, i):
            return i if isinstance(first, int) else (first + i).with_bounds(min_val=0, max_val=TURNS - 1)

        def units_of(k):
            return [min(UNIT, k - j) for j in range(0, k, UNIT)]

        class At:

            def __init__(self, at, parity):
                self.at, self.parity = at, parity

        def each_segment(engine, segment, begins, ends):
            unit = 0
            for strip in range(STRIPS):
                begins(strip)
                if strip == 0:
                    for seg in range(SEGS):
                        windows = []
                        for w in range(seg * SEG, seg * SEG + SEG):
                            windows.append((At(w, w % 2), At(unit, unit % 2), VISITS[w]))
                            unit += len(units_of(VISITS[w]))
                        segment(strip, seg, windows)
                else:
                    seg0 = 0
                    for n, k in RUNS[strip - 1]:
                        with engine.Fori(0, n) as i:
                            w0, u0 = strip * SW + seg0 * SEG, unit
                            segment(strip, i + seg0, [(At(i * SEG + (w0 + j), j % 2), At(i * SEG + (u0 + j), (u0 + j) % 2), k)
                                                      for j in range(SEG)])
                        seg0 += n
                        unit += n * SEG
                ends(strip)

        def visits_upto(w):
            return sum(VISITS[:w])

        @block.sync
        def _(sp):
            sp.dma_start(dst_i, t["dst_t"]).then_inc(loaded, 16)
            sp.dma_start(consts[:], t["consts"]).then_inc(loaded, 16)
            sp.dma_start(visit_plan[:], t["visit_plan"]).then_inc(loaded, 16)
            sp.dma_start(agg[:], t["x_nodes"].rearrange("p b d -> p (b d)")).then_inc(loaded, 16)
            for n in range(2):
                sp.dma_start(conv_w[:, n], t[f"L0_gnn_W{n + 1}"]).then_inc(loaded, 16)
                sp.dma_start(conv_b[:, n:n + 1], t[f"L0_gnn_b{n + 1}"].rearrange("(p a) -> p a", a=1)).then_inc(loaded, 16)
            sp.dma_start(msg_w[:], t["L1_gnn_W1"][0:D, :]).then_inc(loaded, 16)
            sp.dma_start(msg_b[:], t["L1_gnn_b1"].rearrange("(a d) -> a d", a=1).to_broadcast([P, D])).then_inc(loaded, 16)
            sp.dma_start(upd_w[:], t["L1_gnn_W2"].rearrange("(k p) d -> p k d", k=2)).then_inc(loaded, 16)
            sp.dma_start(upd_b[:], t["L1_gnn_b2"].rearrange("(a d) -> a d", a=1).to_broadcast([P, D])).then_inc(loaded, 16)
            for q in range(CQ):
                if q:
                    sp.wait_ge(rows_reduced, q)
                sp.dma_start(rows_i[0:CR, :], t["dst_rows"][:, q]).then_inc(rows_loaded, 16)
            sp.wait_ge(setup_ready, 1)
            for j in range(TC):
                sp.dma_start(edge_w[DE * j:DE * (j + 1), j, :], t["L1_gnn_W1"][D:D + DE, :]).then_inc(edge_w_loaded, 16)
            sp.wait_ge(rows_reduced, CQ)
            sp.dma_start(tiles_dram[0].rearrange("(p q) -> p q", p=CR), row_min[0:CR, :]).then_inc(tiles_stored, 16)
            sp.dma_start(tiles_dram[1].rearrange("(p q) -> p q", p=CR), row_max[0:CR, :]).then_inc(tiles_stored, 16)
            sp.wait_ge(tiles_stored, 32)
            sp.dma_start(tile_min, tiles_dram[0:1, :].to_broadcast([P, NT])).then_inc(tiles_loaded, 16)
            sp.dma_start(tile_max, tiles_dram[1:2, :].to_broadcast([P, NT])).then_inc(tiles_loaded, 16)
            sp.wait_ge(starts_int, 1)
            sp.dma_start(starts_dram.rearrange("(b p) a -> b (p a)", p=P), starts_i[:]).then_inc(starts_stored, 16)

            def store_table(n):
                table = tables[n].rearrange("(g b p) d -> g p b d", b=GB, p=P)
                if n == 0:
                    sp.sem_inc(G["tab_free"], 1)
                with sp.Fori(0, NG) as g:
                    sp.wait_ge(G["tab"], group(n, g) + 1)
                    sp.dma_start(table[bass.ds(g, 1)].rearrange("a p b d -> (a p) b d"), tab[:]).then_inc(G["tab_stored"], 16)
                    sp.wait_ge(G["tab_stored"], group(n, g) * 16 + 16)
                    sp.sem_inc(G["tab_free"], 1)

            def load_edges(e, first, turns, messages=False):
                def load_indices(at, h):
                    sp.dma_start(idx[:, h], t["src_t"][:, bass.ds(at * (SLOTS * TC) + h * HALF * TC, HALF * TC)]
                                 ).then_inc(e["idx_" + "ab"[h]], 16)

                for h in range(2):
                    load_indices(turn_at(first, 0), h)
                with sp.Fori(0, turns) as i:
                    for h in range(2):
                        if messages:
                            sp.wait_ge(e["added"], i * SLOTS + HALF * (h + 1))
                            sp.dma_start(attr[:, h * HALF:(h + 1) * HALF],
                                         t["attr_t"][:, bass.ds(turn_at(first, i) * SLOTS + h * HALF, HALF)]
                                         ).then_inc(attr_loaded[h], 16)
                    for h in range(2):
                        for s in range(h * HALF, (h + 1) * HALF, e["apart"]):
                            sp.wait_ge(e["gathered"][s // e["apart"]], (i + 1) * (16 * TC * e["apart"]))
                        load_indices(turn_at(first, i) + 1, h)
                for h in range(2):
                    sp.wait_ge(e["idx_" + "ab"[h]], turns * 16 + 16)
                    sp.sem_inc(held["sp"], 1)

            def shared(n):
                first = sp.value_load(turns_i[0:1, 0:1], min_val=0, max_val=TURNS - 1)
                turns = sp.value_load(turns_i[0:1, 1:2], min_val=1, max_val=TURNS)
                load_edges(shared_passes[n], first, turns)

            def full(n):
                sp.wait_ge(full_ready, n + 1)
                sp.dma_start(agg[:], own_dram).then_inc(own_restored, 16)
                load_edges(full_passes[n], 0, TURNS)

            for n in range(2):
                store_table(n)
                sp.wait_ge(G["own"], NG * (n + 1))
                sp.dma_start(own_dram, agg[:]).then_inc(own_stored, 16)
                if n == 0:
                    sp.wait_ge(tables_ready, 1)
                    shared(n)
                    sp.wait_ge(flag_ready, 1)
                    flagged = sp.value_load(flag[0:1, 0:1], min_val=0, max_val=1)
                    with sp.If(flagged > 0):
                        full(n)
                else:
                    with sp.If(flagged > 0):
                        full(n)
                    with sp.Else():
                        shared(n)
            sp.wait_ge(dense_done, 2)
            sp.dma_start(h2, t["x_nodes"].rearrange("p b d -> p (b d)")).then_inc(x_loaded, 16)
            store_table(2)
            load_edges(msg_pass, 0, TURNS, True)

            rows_out = out.rearrange("(g b p) d -> g p b d", b=GB, p=P)
            sp.sem_inc(fin["out_free"], 1)
            with sp.Fori(0, NG) as g:
                sp.wait_ge(fin["out"], g + 1)
                sp.dma_start(rows_out[bass.ds(g, 1)].rearrange("a p b d -> (a p) b d"), normed[:]).then_inc(fin["stored"], 16)
                sp.wait_ge(fin["stored"], g * 16 + 16)
                sp.sem_inc(fin["out_free"], 1)
            sp.wait_ge(fin["stored"], 16 * NG)

        @block.gpsimd
        def _(pool):
            def gather(e, n, turns):
                with pool.Fori(0, turns) as i:
                    for h in range(2):
                        pool.wait_ge(e["idx_" + "ab"[h]], i * 16 + 16)
                        for k in range(HALF * TC):
                            s, j = h * HALF + k // TC, k % TC
                            if j == 0:
                                pool.wait_ge(e["added"], i * SLOTS + s + 1)
                                pool.sem_inc(held["pool"])
                            nc.gpsimd.indirect_dma_start(
                                rows[:, s, j * D:(j + 1) * D], None, tables[n],
                                bass.IndirectOffsetOnAxis(ap=idx[:, h, k:k + 1], axis=0),
                            ).then_inc(e["gathered"][s // e["apart"]], 16)

            pool.wait_ge(loaded, 16 * N_LOADS)
            pool.wait_ge(starts_stored, 16)
            for b in range(VB):
                nc.gpsimd.indirect_dma_start(
                    visit_start[:, b:b + 1], None, starts_dram,
                    bass.IndirectOffsetOnAxis(ap=visit_plan[:, 0, b:b + 1], axis=0)).then_inc(starts_gathered, 16)
            pool.wait_ge(visit_rows_ready, 1)
            for b in range(VB):
                nc.gpsimd.indirect_dma_start(
                    visit_edges[:, b].rearrange("p k e -> p (k e)"), None, t["edge_rows"],
                    bass.IndirectOffsetOnAxis(ap=visit_row[:, b:b + 1], axis=0)).then_inc(visits_gathered, 16)
            for n in range(2):
                pool.wait_ge(G["tab_stored"], 16 * NG * (n + 1))
                if n == 0:
                    pool.wait_ge(tables_ready, 1)
                    turns = pool.value_load(turns_i[0:1, 1:2], min_val=1, max_val=TURNS)
                    gather(shared_passes[n], n, turns)
                    pool.wait_ge(flag_ready, 1)
                    flagged = pool.value_load(flag[0:1, 0:1], min_val=0, max_val=1)
                    with pool.If(flagged > 0):
                        gather(full_passes[n], n, TURNS)
                else:
                    with pool.If(flagged > 0):
                        gather(full_passes[n], n, TURNS)
                    with pool.Else():
                        gather(shared_passes[n], n, turns)
            pool.wait_ge(G["tab_stored"], 16 * NG * 3)
            gather(msg_pass, 2, TURNS)

        @block.tensor
        def _(pe):
            mm = nc.tensor.matmul
            pe.wait_ge(loaded, 16 * N_LOADS)
            pe.wait_ge(setup_ready, 1)
            mm(ps_node[:, 0:NB], zero_bf[:], zero_bf[:, 0:NB], start=True, stop=False, skip_group_check=True)
            pe.sem_inc(hist_used, 2)
            with pe.Fori(0, HSTEPS) as i:
                for s in range(2):
                    pe.wait_ge(lo_ready, i * 2 + s + 1)
                    pe.wait_ge(hi_ready, i * 2 + s + 1)
                    for j in range(HT):
                        last = mm(ps_node[:, 0:NB], hot_lo[:, s, j], hot_hi[:, s, j], start=False, stop=False,
                                  skip_group_check=True)
                    last.then_inc(hist_used, 1)
            mm(ps_node[:, 0:NB], zero_bf[:], zero_bf[:, 0:NB], start=False, stop=True,
               skip_group_check=True).then_inc(count_ready, 1)
            pe.wait_ge(count_copied, 1)
            mm(ps_turn[:, 0:NB], above, count[:], start=True, stop=True).then_inc(before_ready, 1)
            mm(ps_feat[:, 0:NB], ones[:], count[:], start=True, stop=True).then_inc(before_ready, 1)
            pe.wait_ge(starts_ready, 1)
            nc.tensor.transpose(ps_sum[0][0:NB, 0:P], starts[:, 0], ident).then_inc(starts_turned, 1)
            pe.wait_ge(visits_split, 1)
            for b in range(VB):
                if b >= 2:
                    pe.wait_ge(visits_copied, b - 1)
                for k in range(2):
                    last = nc.tensor.transpose(ps_sum[b % 2][:, k * P:(k + 1) * P], split_edges[:, b, k], ident)
                last.then_inc(visits_turned, 1)

            def turn(to, of):
                for b in range(GB):
                    last = nc.tensor.transpose(to[:, b * P:(b + 1) * P], of(b), ident)
                return last

            def node_phase(n):
                with pe.Fori(0, NG) as g:
                    k = group(n, g)
                    if n:
                        pe.wait_ge(G["diag"], k - NG + 1)
                        mm(ps_pre[1][:], ones[:], diag.rearrange("p b n -> p (b n)"), start=True, stop=True).then_inc(G["row"], 1)
                    if n == 2:
                        pe.wait_ge(G["shifted"], g + 1)
                        turn(ps_pre[0], lambda b: feat_agg[:, b * P:(b + 1) * P]).then_inc(G["back"], 1)
                    if n != 1:
                        pe.wait_ge(G["normed"], g + 1 + NG * (n // 2))
                        turn(ps_turn, lambda b: normed[:, b]).then_inc(G["turned"], 1)
                    pe.wait_ge(G["feat"], k + 1)
                    pe.wait_ge(G["freed"], k + 1)
                    w = conv_w[:, n] if n < 2 else msg_w[:]
                    for b in range(GB):
                        last = mm(ps_node[:, b * D:(b + 1) * D], feat[:, b * P:(b + 1) * P], w, start=True, stop=True)
                    last.then_inc(G["products"], 1)
                    if n < 2:
                        pe.wait_ge(G["tab"], k + 1)
                        turn(ps_feat, lambda b: tab[:, b]).then_inc(G["own_turned"], 1)

            def sum_chunk(e, i, s, lhs):
                c = i * SLOTS + s
                if e["every"]:
                    more = pe.value_load(chunk_window[0:1, 1, bass.ds(c, 1)], min_val=0, max_val=NB)
                    with pe.If(more > 0):
                        a = pe.value_load(chunk_window[0:1, 2, bass.ds(c, 1)], min_val=0, max_val=NCH * NB)
                        with pe.Fori(0, more) as k:
                            pe.wait_ge(e["x_onehot"], a + k + 2)
                            pe.wait_ge(e["x_added"], a + k + 1)
                            for j in range(TC):
                                last = mm(ps_extra[:, 0:P], lhs[:, j * D:(j + 1) * D], onehot_x[:, j], start=(j == 0), stop=(j == TC - 1))
                            last.then_inc(e["x_summed"], 1)
                pe.wait_ge(e["added"], c + 7)
                pe.wait_ge(e["onehot"], c + 1)
                for j in range(TC):
                    last = mm(ps_sum[s % 2][:, 0:P], lhs[:, j * D:(j + 1) * D], onehot[:, s % 2, j], start=(j == 0), stop=(j == TC - 1))
                last.then_inc(e["summed"], 1)

            def edge_turn(e, i, messages=False):
                def before(s):
                    if s % e["apart"] == 0:
                        pe.wait_ge(e["gathered"][s // e["apart"]], (i + 1) * (16 * TC * e["apart"]))
                    if messages:
                        if s % HALF == 0:
                            pe.wait_ge(attr_loaded[s // HALF], i * 16 + 16)
                        pe.wait_ge(msgs_ready, i * SLOTS + s + 1)
                        mm(ps_pre[s % 2][:], attr[:, s], edge_w[:].rearrange("p j d -> p (j d)"), start=True, stop=False)
                        mm(ps_pre[s % 2][:], ident, rows[:, s], start=False, stop=True).then_inc(pre_ready, 1)

                def after(s):
                    if messages:
                        pe.wait_ge(msgs_ready, i * SLOTS + s + 3)
                    sum_chunk(e, i, s, msgs[:, s % 2] if messages else rows[:, s])

                before(0)
                for s in range(1, SLOTS):
                    before(s)
                    after(s - 1)
                after(SLOTS - 1)

            def build_window(w, unit, k):
                bank = ps_pre[w.parity][:, 0:KEYS]
                pe.wait_ge(C["evacuated"], w.at + 1)
                for u, n in enumerate(units_of(k)):
                    par = (unit.parity + u) % 2
                    pe.wait_ge(C["hot"], unit.at + (u + 1))
                    for j in range(n):
                        ins = mm(bank, hot_src[:, par, j], hot_key[:, par, j], start=(u == 0 and j == 0),
                                 stop=(u * UNIT + j == k - 1), skip_group_check=True)
                    ins.then_inc(C["built"], 1)

            def strip_bank(buf):
                return (ps_feat if buf else ps_node)[:, 0:STRIP]

            def apply(buf, h, first=False, last=False):
                for k in range(PARTS):
                    ins = mm(strip_bank(buf), parts_at(h, k), counts_at(buf, h), start=first and k == 0,
                             stop=last and k == PARTS - 1, skip_group_check=True)
                return ins

            def parts_at(h, k):
                if isinstance(h, int):
                    return parts[:, h, k]
                return parts[:, bass.ds(h, 1), k].rearrange("p a d -> p (a d)")

            def counts_at(buf, h):
                if isinstance(h, int):
                    return counts[buf][:, h]
                return counts[buf][:, bass.ds(h, 1)].rearrange("p a d -> p (a d)")

            def shared(n):
                e = shared_passes[n]
                turns = pe.value_load(turns_i[0:1, 1:2], min_val=1, max_val=TURNS)
                pe.sem_inc(e["summed"], 2)
                pe.wait_ge(G["part"], NG * PARTS * (n + 1))

                def turn_beside(i):
                    with pe.If(turns > i):
                        edge_turn(e, i)

                if n == 0:
                    pe.sem_inc(C["built"], 2)

                    def segment(strip, seg, windows):
                        other = 1 - strip % 2
                        for j, (w, unit, k) in enumerate(windows):
                            build_window(w, unit, k)
                            if strip:
                                for h in (j + j // 2, ) if j % 2 else (j + j // 2, j + j // 2 + 1):
                                    apply(other, seg * 12 + h + (j % 2))
                        turn_beside(seg + strip * SEGS)

                    def strip_begins(strip):
                        if strip:
                            pe.wait_ge(C["evacuated"], strip * SW + 2)
                            pe.wait_ge(strip_added[1 - strip % 2], (strip + 1) // 2)
                            apply(1 - strip % 2, SB - 1, first=True)

                    def strip_ends(strip):
                        if strip:
                            mm(strip_bank(1 - strip % 2), zero_bf[:], zero_strip[:], start=False, stop=True,
                               skip_group_check=True).then_inc(applied[1 - strip % 2], 1)

                    each_segment(pe, segment, strip_begins, strip_ends)
                    pe.wait_ge(C["evacuated"], NW + 2)
                    pe.wait_ge(strip_added[1], STRIPS // 2)
                    for h in range(SB):
                        ins = apply(1, h, first=(h == 0), last=(h == SB - 1))
                    ins.then_inc(applied[1], 1)
                else:
                    with pe.Fori(0, STRIPS // 2) as u:
                        for buf in range(2):
                            pe.wait_ge(C["loaded_" + "ab"[buf]], u * 16 + 16)
                            pe.wait_ge(strip_added[buf], u + (STRIPS // 2 + 1))
                            for seg in range(SEGS):
                                last = seg == SEGS - 1
                                for h in range(seg * 12, seg * 12 + 12 + last):
                                    ins = apply(buf, h, first=(h == 0), last=(h == SB - 1))
                                if last:
                                    ins.then_inc(applied[buf], 1)
                                turn_beside(u * (2 * SEGS) + (buf * SEGS + seg))
                with pe.If(turns > STRIPS * SEGS):
                    with pe.Fori(STRIPS * SEGS, turns) as i:
                        edge_turn(e, i)
                pe.nop()

            def full(n):
                pe.sem_inc(full_passes[n]["summed"], 2)
                with pe.Fori(0, TURNS) as i:
                    edge_turn(full_passes[n], i)

            node_phase(0)
            pe.wait_ge(tables_ready, 1)
            shared(0)
            pe.wait_ge(most_ready, 1)
            mm(ps_turn[0:1, 0:P], found[:, 0:1], ident, start=True, stop=True).then_inc(most_turned, 1)
            mm(ps_extra[0:1, 0:1], found[:, 3:4], ones[:, 0:1], start=True, stop=True).then_inc(most_turned, 1)
            pe.wait_ge(flag_ready, 1)
            flagged = pe.value_load(flag[0:1, 0:1], min_val=0, max_val=1)
            with pe.If(flagged > 0):
                full(0)
            node_phase(1)
            with pe.If(flagged > 0):
                full(1)
            with pe.Else():
                shared(1)
            node_phase(2)
            pe.sem_inc(msg_pass["summed"], 2)
            pe.wait_ge(edge_w_loaded, 16 * TC)
            with pe.Fori(0, TURNS) as i:
                edge_turn(msg_pass, i, True)

            with pe.Fori(0, NG) as g:
                pe.wait_ge(fin["copied"], g * 2 + 2)
                pe.wait_ge(fin["free"], g + 1)
                for b in range(GB):
                    mm(ps_node[:, b * D:(b + 1) * D], feat[:, b * P:(b + 1) * P], upd_w[:, 0], start=True, stop=True)
                for b in range(GB):
                    last = mm(ps_feat[:, b * D:(b + 1) * D], feat_agg[:, b * P:(b + 1) * P], upd_w[:, 1], start=True, stop=True)
                last.then_inc(fin["multiplied"], 1)

        @block.scalar
        def _(act):
            def hold(s, value):
                act.wait_ge(s, value)
                act.sem_inc(held["act"], 1)

            act.wait_ge(degree_ready, 1)
            nc.scalar.activation(degree_root[:], degree[:], ACT.Sqrt).then_inc(root_ready, 1)

            def node_phase(n):
                with act.Fori(0, NG) as g:
                    k = group(n, g)
                    cols = bass.ds(g * GN, GN)
                    if n == 2:
                        act.wait_ge(G["scaled"], NG + g + 1)
                        nc.scalar.activation(feat_agg[:], scaled[:], ACT.Identity, bias=conv_b[:, 1:2]).then_inc(G["shifted"], 1)
                    if n != 1:
                        act.wait_ge(G["moments"], g + 1 + NG * (n // 2))
                        nc.scalar.activation(std[:], moments[:, :, 1], ACT.Sqrt, bias=eps[:]).then_inc(G["std"], 1)
                        act.wait_ge(G["turned"], g + 1 + NG * (n // 2))
                        act.wait_ge(G["freed"], k + 1)
                        nc.scalar.activation(feat[:], ps_turn[:], ACT.Relu).then_inc(G["feat"], 1)
                    else:
                        act.wait_ge(G["scaled"], g + 1)
                        act.wait_ge(G["freed"], k + 1)
                        nc.scalar.activation(feat[:], scaled[:], ACT.Relu, bias=conv_b[:, 0:1]).then_inc(G["feat"], 1)
                    if n == 2:
                        nc.scalar.activation(h2[:, cols], ps_turn[:], ACT.Relu).then_inc(G["h2"], 1)
                    else:
                        blocks = bass.ds(g * GB, GB)
                        hold(G["tab"], k + 1)
                        nc.scalar.activation(parts[:, blocks, 0], tab[:], ACT.Copy).then_inc(G["part"], 1)
                        hold(G["own_turned"], k + 1)
                        nc.scalar.activation(agg[:, cols], ps_feat[:], ACT.Copy).then_inc(G["own"], 1)
                        for j in range(1, PARTS):
                            hold(G["rest"], k * 2 + j)
                            nc.scalar.activation(parts[:, blocks, j], rest, ACT.Copy).then_inc(G["part"], 1)

            def segment(strip, seg, windows):
                for j, (w, unit, k) in enumerate(windows):
                    hold(C["built"], unit.at + (len(units_of(k)) + 2))
                    nc.scalar.activation(
                        counts[strip % 2][:, :, bass.ds(seg * (SEG * W) + j * W, W)],
                        ps_pre[w.parity][:, 0:KEYS].rearrange("p (d h) -> p h d", h=SB), ACT.Copy,
                        accum_out=row_sums[:, bass.ds(w.at, 1)]).then_inc(C["evacuated"], 1)

            def strip_begins(strip):
                if strip >= 2:
                    free_counts(strip % 2, strip // 2)

            def strip_ends(strip):
                act.wait_ge(C["evacuated"], strip * SW + (SW + 2))
                act.dma_start(counts_dram[strip], counts[strip % 2].rearrange("p h d -> p (h d)")
                              ).then_inc(C["stored_" + "ab"[strip % 2]], 16)

            def strip_dram(strip):
                return counts_dram[bass.ds(strip, 1)].rearrange("a p c -> (a p) c")

            def free_counts(buf, uses):
                act.wait_ge(applied[buf], uses)
                act.wait_ge(C["stored_" + "ab"[buf]], uses * 16)
                act.sem_inc(held["act"], 1)

            def shared(n):
                if n == 0:
                    act.sem_inc(C["evacuated"], 2)
                    each_segment(act, segment, strip_begins, strip_ends)
                else:
                    for buf in range(2):
                        act.wait_ge(C["stored_a"], 8 * STRIPS)
                        act.wait_ge(C["stored_b"], 8 * STRIPS)
                        act.wait_ge(applied[buf], STRIPS // 2)
                        act.dma_start(counts[buf].rearrange("p h d -> p (h d)"), counts_dram[buf]).then_inc(C["loaded_" + "ab"[buf]], 16)
                    with act.Fori(1, STRIPS // 2) as u:
                        for buf in range(2):
                            act.wait_ge(applied[buf], u + STRIPS // 2)
                            act.dma_start(counts[buf].rearrange("p h d -> p (h d)"), strip_dram(u * 2 + buf)
                                          ).then_inc(C["loaded_" + "ab"[buf]], 16)

            node_phase(0)
            shared(0)
            act.wait_ge(flag_ready, 1)
            flagged = act.value_load(flag[0:1, 0:1], min_val=0, max_val=1)
            node_phase(1)
            with act.If(flagged < 1):
                shared(1)
            act.wait_ge(x_loaded, 16)
            node_phase(2)
            act.wait_ge(G["h2"], NG)
            e = msg_pass
            act.sem_inc(msgs_ready, 2)
            with act.Fori(0, TURNS) as i:
                for s in range(SLOTS):
                    act.wait_ge(pre_ready, i * SLOTS + s + 1)
                    act.wait_ge(e["summed"], i * SLOTS + s + 1)
                    nc.scalar.activation(msgs[:, s % 2], ps_pre[s % 2][:], ACT.Relu).then_inc(msgs_ready, 1)
            act.wait_ge(e["added"], SLOTS + NCH)
            with act.Fori(0, NG) as g:
                hold(fin["free"], g + 1)
                nc.scalar.activation(feat[:], h2[:, bass.ds(g * GN, GN)], ACT.Copy).then_inc(fin["copied"], 1)
                nc.scalar.activation(feat_agg[:], agg[:, bass.ds(g * GN, GN)], ACT.Copy).then_inc(fin["copied"], 1)

        @block.vector
        def _(dve):
            v = nc.vector
            steps = [0]

            def link(ins):
                steps[0] += 1
                ins.then_inc(dve_did, 1)
                dve.wait_ge(dve_did, steps[0])

            def hold(s, value):
                dve.wait_ge(s, value)
                dve.sem_inc(held["dve"], 1)

            v.memset(edge_w[:], 0.0).then_inc(dve_did, 1)
            v.memset(ones[:], 1.0).then_inc(dve_did, 1)
            v.memset(zero_bf[:], 0.0).then_inc(dve_did, 1)
            v.memset(zero_strip[:], 0.0).then_inc(dve_did, 1)
            steps[0] = 4
            link(v.memset(eps[:], EPS))
            dve.sem_inc(setup_ready, 1)
            dve.wait_ge(loaded, 16 * N_LOADS)
            v.tensor_copy(iota_bf[:], iota)
            v.tensor_copy(iota_key[:], key_iota)
            link(v.tensor_single_scalar(part_i, dst_i, P - 1, ALU.bitwise_and))
            link(v.tensor_copy(dst_lo, part_i))
            link(v.tensor_single_scalar(part_i, dst_i, 7, ALU.arith_shift_right))
            v.tensor_copy(dst_hi, part_i).then_inc(parts_split, 1)
            dve.wait_ge(parts_split, 1)
            with dve.Fori(0, HSTEPS) as i:
                for s in range(2):
                    dve.wait_ge(hist_used, i * 2 + s + 1)
                    for hot, of, n, ready in ((hot_lo, dst_lo, P, lo_ready), (hot_hi, dst_hi, NB, hi_ready)):
                        v.tensor_tensor(hot[:, s], iota_bf[:, None, 0:n].to_broadcast([P, HT, n]),
                                        of[:, bass.ds(i * (2 * HT) + s * HT, HT)].unsqueeze(2).to_broadcast([P, HT, n]),
                                        ALU.is_equal).then_inc(ready, 1)
            for q in range(CQ):
                dve.wait_ge(rows_loaded, 16 * (q + 1))
                row = rows_i[0:CR, :].rearrange("p (t e) -> p t e", t=TC)
                v.tensor_reduce(row_min[0:CR, q * TC:(q + 1) * TC], row, AX.X, ALU.min).then_inc(dve_did, 1)
                v.tensor_reduce(row_max[0:CR, q * TC:(q + 1) * TC], row, AX.X, ALU.max).then_inc(dve_did, 1)
                steps[0] += 2
                dve.wait_ge(dve_did, steps[0])
                dve.sem_inc(rows_reduced, 1)
            dve.wait_ge(count_ready, 1)
            link(v.tensor_copy(count[:], ps_node[:, 0:NB]))
            dve.sem_inc(count_copied, 1)
            dve.wait_ge(before_ready, 2)
            link(v.tensor_copy(starts[:, 1], ps_feat[:, 0:NB]))
            link(v.tensor_tensor_scan(starts[:, 2], starts[:, 1], starts[:, 1], 0.0, ALU.add, ALU.bypass))
            link(v.tensor_tensor(starts[:, 2], starts[:, 2], starts[:, 1], ALU.subtract))
            v.tensor_tensor(starts[:, 0], starts[:, 2], ps_turn[:, 0:NB], ALU.add).then_inc(starts_ready, 1)
            dve.wait_ge(starts_turned, 1)
            v.tensor_copy(starts_i[:], ps_sum[0][0:NB, 0:P]).then_inc(starts_int, 1)
            dve.wait_ge(starts_gathered, 16 * VB)
            link(v.tensor_single_scalar(visit_start[:], visit_start[:], 4, ALU.arith_shift_right))
            v.tensor_tensor(visit_row[:], visit_start[:], visit_plan[:, 1], ALU.add).then_inc(visit_rows_ready, 1)
            v.tensor_scalar(degree[:], count[:], 1.0, None, ALU.add).then_inc(degree_ready, 1)
            link(v.tensor_scalar(atleast1[:], count[:], 1.0, None, ALU.max))
            link(v.reciprocal(inv_count[:], atleast1[:]))
            dve.wait_ge(root_ready, 1)
            link(v.reciprocal(dinv[:], degree_root[:]))
            dve.wait_ge(tiles_loaded, 32)
            by_chunk = [a.rearrange("p (c t) -> p c t", t=TC) for a in (tile_min, tile_max, dst_i, dst_rel[:])]
            chunk_min = part_i[:, 0:NCH]
            chunk_max = part_i[:, NCH:2 * NCH]
            link(v.tensor_reduce(chunk_min, by_chunk[0], AX.X, ALU.min))
            link(v.tensor_reduce(chunk_max, by_chunk[1], AX.X, ALU.max))
            link(v.tensor_tensor(by_chunk[3], by_chunk[2], chunk_min.unsqueeze(2).to_broadcast([P, NCH, TC]), ALU.subtract))
            before = part_i[:].bitcast(F32)
            link(v.tensor_copy(chunk_window[:, 0], chunk_min[0:1]))
            link(v.tensor_tensor(chunk_max[0:1], chunk_max[0:1], chunk_min[0:1], ALU.subtract))
            link(v.tensor_single_scalar(chunk_window[:, 1], chunk_max[0:1], 7, ALU.arith_shift_right))

            def counted_ahead(table, f):
                link(v.tensor_copy(f, table[:, 1]))
                link(v.tensor_tensor_scan(f, f, f, 0.0, ALU.add, ALU.bypass))
                link(v.tensor_tensor(table[:, 2], f, table[:, 1], ALU.subtract))

            counted_ahead(chunk_window, upto[:])
            link(v.tensor_scalar(before, dst_i, float(DENSE), MASKED, ALU.is_lt, ALU.mult))
            link(v.tensor_tensor(dst_rel[:], dst_rel[:], before, ALU.add))
            far = tile_max.bitcast(F32)
            link(v.tensor_copy(far, tile_max))
            link(v.tensor_tensor_scan(far, far, far, -1.0, ALU.max, ALU.bypass))
            link(v.tensor_scalar(before, far, float(DENSE), None, ALU.is_lt))
            link(v.tensor_reduce(before_dense[:, 0:1], before, AX.X, ALU.add))
            link(v.tensor_copy(turns_i[:, 2:3], before_dense[:, 0:1]))
            link(v.tensor_single_scalar(turns_i[:, 3:4], turns_i[:, 2:3], 5, ALU.arith_shift_right))
            link(v.tensor_copy(before_dense[:, 1:2], turns_i[:, 3:4]))
            link(v.tensor_scalar(before_dense[:, 0:1], before_dense[:, 1:2], float(TURNS - 1), None, ALU.min))
            link(v.tensor_copy(turns_i[:, 0:1], before_dense[:, 0:1]))
            link(v.tensor_scalar(before_dense[:, 1:2], before_dense[:, 0:1], -1.0, float(TURNS), ALU.mult, ALU.add))
            link(v.tensor_copy(turns_i[:, 1:2], before_dense[:, 1:2]))
            dve.wait_ge(visits_gathered, 16 * VB)
            block_i = part_columns.rearrange("p (v e) -> p v e", v=VB)
            link(v.tensor_single_scalar(block_i, visit_edges[:, :, 0], P - 1, ALU.bitwise_and))
            link(v.tensor_copy(split_edges[:, :, 0], block_i))
            link(v.tensor_single_scalar(block_i, visit_edges[:, :, 0], 7, ALU.arith_shift_right))
            link(v.tensor_copy(split_edges[:, :, 1], block_i))
            link(v.scalar_tensor_tensor(out=split_edges[:, :, 1], in0=visit_edges[:, :, 1], scalar=float(SB),
                                        in1=split_edges[:, :, 1], op0=ALU.mult, op1=ALU.add))
            link(v.tensor_tensor(split_edges[:, :, 1], split_edges[:, :, 1],
                                 visit_key.unsqueeze(2).to_broadcast([P, VB, P]), ALU.add))
            dve.sem_inc(visits_split, 1)
            for b in range(VB):
                dve.wait_ge(visits_turned, b + 1)
                last = v.tensor_copy(visit[:, b * P:(b + 1) * P].rearrange("p v k -> p k v"),
                                     ps_sum[b % 2][:, 0:2 * P].rearrange("p (k v) -> p k v", k=2))
                last.then_inc(visits_copied, 1)
            dve.wait_ge(visits_copied, VB)
            dve.sem_inc(tables_ready, 1)

            def layernorm(block_of, n, g):
                k = g + NG * (n // 2)
                for b in range(GB):
                    v.bn_stats(stats[:, b], block_of(b)).then_inc(G["stats"], 1)
                hold(G["stats"], k * GB + GB)
                for b in range(GB):
                    last = v.bn_aggr(moments[:, b], stats[:, b])
                last.then_inc(G["moments"], 1)
                dve.wait_ge(G["moments"], k + 1)
                dve.wait_ge(G["std"], k + 1)
                link_rstd = v.reciprocal(rstd[:], std[:])
                link_rstd.then_inc(rstd_ready, 1)
                dve.wait_ge(rstd_ready, k + 1)
                for b in range(GB):
                    last = v.tensor_scalar(normed[:, b], block_of(b), moments[:, b, 0:1], rstd[:, b:b + 1],
                                           ALU.subtract, ALU.mult)
                last.then_inc(G["normed"], 1)

            def block_of(a, g):
                return lambda b: a[:, bass.ds(g * GN + b * P, P)]

            def node_phase(n):
                if n == 0:
                    dve.sem_inc(G["freed"], 1)
                with dve.Fori(0, NG) as g:
                    k = group(n, g)
                    cols = bass.ds(g * GN, GN)
                    dinv_g = dinv[:, bass.ds(g * GB, GB)].unsqueeze(2)
                    if n == 0:
                        layernorm(block_of(agg, g), n, g)
                    else:
                        v.tensor_tensor(diag, ident[:, None, :].to_broadcast([P, GB, P]), dinv_g.to_broadcast([P, GB, P]),
                                        ALU.mult).then_inc(G["diag"], 1)
                        dve.wait_ge(G["row"], k - NG + 1)
                        v.tensor_tensor(scaled[:], agg[:, cols], ps_pre[1][:], ALU.mult).then_inc(G["scaled"], 1)
                    if n == 2:
                        x1g = region_b[:, cols]
                        dve.wait_ge(G["back"], g + 1)
                        v.tensor_tensor(x1g, h2[:, cols], ps_pre[0][:], ALU.add).then_inc(G["x1"], 1)
                        hold(G["x1"], g + 1)
                        layernorm(block_of(region_b, g), n, g)
                    dve.wait_ge(G["products"], k + 1)
                    dve.wait_ge(G["tab_free"], k + 1)
                    nodes = ps_node[:].rearrange("p (b d) -> p b d", b=GB)
                    if n < 2:
                        v.tensor_tensor(tab[:], nodes, dinv_g.to_broadcast([P, GB, D]), ALU.mult).then_inc(G["tab"], 1)
                        blocks = bass.ds(g * GB, GB)
                        dve.wait_ge(G["tab"], k + 1)
                        for j in range(PARTS - 1):
                            dve.wait_ge(G["part"], k * PARTS + j + 1)
                            v.tensor_tensor(rest, rest if j else tab[:], parts[:, blocks, j], ALU.subtract).then_inc(G["rest"], 1)
                            dve.wait_ge(G["rest"], k * 2 + j + 1)
                        dve.wait_ge(G["part"], k * PARTS + PARTS)
                        dve.wait_ge(G["own"], k + 1)
                    else:
                        v.tensor_tensor(tab[:], nodes, msg_b[:, None, :].to_broadcast([P, GB, D]), ALU.add).then_inc(G["tab"], 1)
                        dve.wait_ge(G["tab"], k + 1)
                        dve.wait_ge(G["h2"], g + 1)
                    dve.sem_inc(G["freed"], 1)

            def edge_turn(e, i, first):
                bases = [None] * SLOTS

                def hot(s):
                    at = turn_at(first, i) * SLOTS + s
                    bases[s] = dve.value_load(chunk_window[0:1, 0, bass.ds(at, 1)], min_val=0, max_val=NP - P)
                    v.tensor_tensor(onehot[:, s % 2], iota[:, None, :].to_broadcast([P, TC, P]),
                                    dst_rel[:, bass.ds(at * TC, TC)].unsqueeze(2).to_broadcast([P, TC, P]),
                                    ALU.is_equal).then_inc(e["onehot"], 1)

                def add(s):
                    c = i * SLOTS + s
                    at = turn_at(first, i) * SLOTS + s
                    if e["every"]:
                        more = dve.value_load(chunk_window[0:1, 1, bass.ds(at, 1)], min_val=0, max_val=NB)
                        with dve.If(more > 0):
                            a = dve.value_load(chunk_window[0:1, 2, bass.ds(at, 1)], min_val=0, max_val=NCH * NB)
                            v.tensor_copy(iota_x[:], iota)
                            dve.drain()
                            with dve.Fori(0, more) as k:
                                v.tensor_scalar(iota_x[:], iota_x[:], float(P), None, ALU.add)
                                dve.drain()
                                v.tensor_tensor(onehot_x[:], iota_x[:, None, :].to_broadcast([P, TC, P]),
                                                dst_rel[:, bass.ds(at * TC, TC)].unsqueeze(2).to_broadcast([P, TC, P]),
                                                ALU.is_equal).then_inc(e["x_onehot"], 1)
                                dve.wait_ge(e["x_summed"], a + k + 1)
                                w = agg[:, bass.ds((bases[s] + k * P + P).with_bounds(min_val=0, max_val=NP - P), P)]
                                v.tensor_tensor(w, w, ps_extra[:, 0:P], ALU.add).then_inc(e["x_added"], 1)
                                dve.drain()
                    dve.wait_ge(e["summed"], c + 3)
                    dve.wait_ge(e["added"], c + SLOTS)
                    w = agg[:, bass.ds(bases[s], P)]
                    v.tensor_tensor(w, w, ps_sum[s % 2][:, 0:P], ALU.add).then_inc(e["added"], 1)

                hot(0)
                for s in range(1, SLOTS):
                    hot(s)
                    add(s - 1)
                add(SLOTS - 1)

            def start_pass(e):
                dve.sem_inc(e["added"], SLOTS)
                dve.sem_inc(e["x_added"], 1)
                dve.sem_inc(e["x_onehot"], 1)

            def add_strip(strip, buf, uses):
                dve.wait_ge(applied[buf], uses)
                cols = bass.ds(strip * STRIP, STRIP)
                bank = ps_feat if buf else ps_node
                v.tensor_tensor(agg[:, cols], agg[:, cols], bank[:, 0:STRIP], ALU.add).then_inc(strip_added[buf], 1)
                dve.drain()

            def shared(n):
                e = shared_passes[n]
                start_pass(e)
                first = dve.value_load(turns_i[0:1, 0:1], min_val=0, max_val=TURNS - 1)
                turns = dve.value_load(turns_i[0:1, 1:2], min_val=1, max_val=TURNS)
                dve.wait_ge(own_stored, 16 * (n + 1))

                def turn_beside(strip):
                    with dve.If(turns > strip):
                        edge_turn(e, strip, first)
                        dve.drain()

                if n == 0:
                    dve.sem_inc(strip_added[0], 1)
                    dve.sem_inc(strip_added[1], 1)

                    def segment(strip, seg, windows):
                        if strip:
                            k = windows[0][2]
                            run0 = [i for i, n in enumerate(VISITS[strip * SW:]) if n == k][0] + strip * SW
                            now = visit_now[:, 0:SEG * k]
                            at = visits_upto(strip * SW) + (seg * (SEG * k)) + (
                                visits_upto(run0) - visits_upto(strip * SW) - (run0 - strip * SW) * k)
                            dve.drain()
                            v.tensor_copy(now, visit[:, bass.ds(at, SEG * k)])
                            dve.drain()
                        else:
                            now = visit[:, visits_upto(seg * SEG):visits_upto(seg * SEG + SEG)]
                        at = 0
                        for w, unit, k in windows:
                            for u, n in enumerate(units_of(k)):
                                hold(C["built"], unit.at + (u + 1))
                                par = (unit.parity + u) % 2
                                for j in range(n):
                                    v.tensor_scalar(hot_src[:, par, j], iota_bf[:], now[:, at, 0:1], None, ALU.is_equal)
                                    ins = v.tensor_scalar(hot_key[:, par, j], iota_key[:], now[:, at, 1:2], None, ALU.is_equal)
                                    at += 1
                                ins.then_inc(C["hot"], 1)
                        turn_beside(seg + strip * SEGS)

                    def strip_ends(strip):
                        if strip:
                            add_strip(strip - 1, 1 - strip % 2, (strip + 1) // 2)

                    each_segment(dve, segment, lambda strip: None, strip_ends)
                    add_strip(STRIPS - 1, 1, STRIPS // 2)
                else:
                    with dve.Fori(0, STRIPS // 2) as u:
                        for buf in range(2):
                            for seg in range(SEGS):
                                if seg == SEGS - 1:
                                    add_strip(u * 2 + buf, buf, u + (STRIPS // 2 + 1))
                                turn_beside(u * (2 * SEGS) + (buf * SEGS + seg))
                with dve.If(turns > STRIPS * SEGS):
                    with dve.Fori(STRIPS * SEGS, turns) as i:
                        edge_turn(e, i, first)
                dve.drain()

            def full(n):
                e = full_passes[n]
                start_pass(e)
                if n == 0:
                    unmask()
                dve.wait_ge(own_stored, 16 * (n + 1))
                dve.sem_inc(full_ready, 1)
                dve.wait_ge(own_restored, 16 * (n + 1))
                with dve.Fori(0, TURNS) as i:
                    edge_turn(e, i, 0)
                dve.drain()

            def unmask():
                shift = rows[:].rearrange("p s c -> p (s c)")[:, 0:NT]
                v.tensor_scalar(shift, dst_rel[:], MASKED / 2, -MASKED, ALU.is_lt, ALU.mult)
                dve.drain()
                v.tensor_tensor(dst_rel[:], dst_rel[:], shift, ALU.add)
                dve.drain()

            node_phase(0)
            shared(0)
            dve.wait_ge(C["evacuated"], NW + 2)
            link(v.tensor_reduce(found[:, 0:1], row_sums[:], AX.X, ALU.max))
            link(v.tensor_reduce(found[:, 1:2], row_sums[:], AX.X, ALU.add))
            link(v.tensor_reduce(found[:, 2:3], count[:, 0:DENSE // P], AX.X, ALU.add))
            link(v.tensor_tensor(found[:, 3:4], found[:, 1:2], found[:, 2:3], ALU.subtract))
            dve.sem_inc(most_ready, 1)
            dve.wait_ge(most_turned, 2)
            link(v.tensor_reduce(verdict[:, 0:1], ps_turn[0:1, 0:P], AX.X, ALU.max))
            link(v.tensor_scalar(verdict[:, 0:1], verdict[:, 0:1], EXACT, None, ALU.is_gt))
            link(v.tensor_scalar(verdict[:, 1:2], ps_extra[0:1, 0:1], 0.0, None, ALU.not_equal))
            link(v.tensor_reduce(verdict[:, 2:3], chunk_window[:, 1], AX.X, ALU.max))
            link(v.tensor_reduce(verdict[:, 3:4], verdict[:, 0:3], AX.X, ALU.max))
            link(v.tensor_scalar(flag[:], verdict[:, 3:4], 0.0, None, ALU.is_gt))
            dve.sem_inc(flag_ready, 1)
            flagged = dve.value_load(flag[0:1, 0:1], min_val=0, max_val=1)
            with dve.If(flagged > 0):
                full(0)
            node_phase(1)
            with dve.If(flagged > 0):
                full(1)
            with dve.Else():
                shared(1)
            dve.drain()
            dve.sem_inc(dense_done, 2)
            dve.wait_ge(x_loaded, 16)
            node_phase(2)
            unmask()
            link(v.memset(agg[:], 0.0))
            start_pass(msg_pass)
            with dve.Fori(0, TURNS) as i:
                edge_turn(msg_pass, i, 0)
            dve.wait_ge(msg_pass["added"], NCH + SLOTS)

            dve.sem_inc(fin["free"], 1)
            nodes = ps_node[:].rearrange("p (b d) -> p b d", b=GB)
            sums = ps_feat[:].rearrange("p (b d) -> p b d", b=GB)
            with dve.Fori(0, NG) as g:
                dve.wait_ge(fin["multiplied"], g + 1)
                v.tensor_tensor(tab[:], sums, inv_count[:, bass.ds(g * GB, GB)].unsqueeze(2).to_broadcast([P, GB, D]),
                                ALU.mult).then_inc(fin["steps"], 1)
                dve.wait_ge(fin["steps"], g * 4 + 1)
                v.tensor_tensor(tab[:], nodes, tab[:], ALU.add).then_inc(fin["steps"], 1)
                dve.wait_ge(fin["steps"], g * 4 + 2)
                dve.sem_inc(fin["free"], 1)
                v.tensor_tensor(tab[:], tab[:], upd_b[:, None, :].to_broadcast([P, GB, D]), ALU.add).then_inc(fin["steps"], 1)
                dve.wait_ge(fin["steps"], g * 4 + 3)
                v.tensor_scalar(tab[:], tab[:], 0.0, None, ALU.max).then_inc(fin["steps"], 1)
                dve.wait_ge(fin["steps"], g * 4 + 4)
                dve.wait_ge(fin["out_free"], g + 1)
                v.tensor_tensor(normed[:], x1[:, bass.ds(g * GB, GB)], tab[:], ALU.add).then_inc(fin["out"], 1)
                dve.wait_ge(fin["out"], g + 1)


def kernel(**inputs):
    import numpy as np
    import concourse.bacc as bacc
    from concourse.bass_utils import run_bass_kernel_spmd

    nc = bacc.Bacc("TRN2", target_bir_lowering=False, num_devices=1)
    x = np.zeros((NP, D), np.float32)
    x[:N] = inputs["x"]
    src = np.zeros(EP, np.int32)
    src[:E] = inputs["src"]
    dst = np.full(EP, N, np.int32)
    dst[:E] = inputs["dst"]
    attr = np.zeros((EP, DE), np.float32)
    attr[:E] = inputs["edge_attr_32"]
    long_src = np.concatenate([src, np.zeros(EDGE_ROWS * ROW + P - EP, np.int32)])
    long_dst = np.concatenate([dst, np.full(EDGE_ROWS * ROW + P - EP, N, np.int32)])
    at = ROW * np.arange(EDGE_ROWS)[:, None] + np.arange(P)[None, :]
    visit_of = np.zeros((3, VB * P), np.int32)
    visit_of[0, :sum(VISITS)] = np.repeat(np.arange(NW) * W, VISITS)
    visit_of[1, :sum(VISITS)] = np.concatenate([np.arange(k) for k in VISITS]) * (P // ROW)
    visit_of[2, :sum(VISITS)] = np.repeat(-np.arange(NW) * KEYS, VISITS)
    visit_of = visit_of.reshape(3, VB, P).transpose(2, 0, 1)
    constants = np.concatenate([np.eye(P), np.tile(np.arange(P), (P, 1)), np.tile(np.arange(KEYS), (P, 1)),
                                np.triu(np.ones((P, P)), 1), visit_of[:, 2]], 1).astype(np.float32)
    arrays = {
        "x_nodes": x.reshape(NB, P, D).transpose(1, 0, 2),
        "src_t": np.concatenate([src, np.zeros(SLOTS * CE, np.int32)]).reshape(-1, P).T,
        "dst_t": dst.reshape(NT, P).T,
        "dst_rows": dst.reshape(CR, CQ, CE),
        "attr_t": attr.reshape(NCH, TC, P, DE).transpose(1, 3, 0, 2).reshape(P, NCH, P),
        "consts": constants,
        "visit_plan": visit_of[:, :2],
        "edge_rows": np.concatenate([long_src[at], long_dst[at]], 1),
    }
    for name in ("L0_gnn_W1", "L0_gnn_b1", "L0_gnn_W2", "L0_gnn_b2", "L1_gnn_W1", "L1_gnn_b1", "L1_gnn_W2", "L1_gnn_b2"):
        arrays[name] = inputs[name]
    arrays = {f"{k}_in": np.ascontiguousarray(a) for k, a in arrays.items()}
    t = {k[:-3]: nc.dram_tensor(k, a.shape, mybir.dt.from_np(a.dtype), kind="ExternalInput").ap() for k, a in arrays.items()}
    out = nc.dram_tensor("out_nodes", (NP, D), F32, kind="ExternalOutput").ap()
    build(nc, t, out)
    r = run_bass_kernel_spmd(nc, [arrays], core_ids=[0])
    return r.results[0]["out_nodes"][:N]
```

```python
from contextlib import ExitStack

import concourse.bass as bass
from concourse import mybir

F32 = mybir.dt.float32
BF16 = mybir.dt.bfloat16
F16 = mybir.dt.float16
I32 = mybir.dt.int32
ALU = mybir.AluOpType
ACT = mybir.ActivationFunctionType
AX = mybir.AxisListType

P = 128
N = 6250
E = 200000
D = 128
DE = 32
GB = 4
NG = 13
NB = GB * NG
NP = NB * P
GN = GB * P
TC = 4
CE = TC * P
SLOTS = 8
HALF = SLOTS // 2
NCH = 392
NT = NCH * TC
EP = NT * P
TURNS = NCH // SLOTS
CR = 98
CQ = NCH // CR
CT = CE * CQ // P
HT = 8
HSTEPS = NT // (2 * HT)
W = 8
STRIP = 256
SW = STRIP // W
STRIPS = 6
IN_COUNTS = (STRIPS, 2 * STRIPS)
NW = STRIPS * SW
SEG = 8
SEGS = SW // SEG
BANKS = 4
UNIT = 6
ROW = 16
FIRST_VISITS = (59, 26, 20, 17, 15, 14, 13, 12, 11, 11, 10, 10, 10, 9, 9, 9, 9, 8, 8, 8, 8, 8, 7, 7, 7, 7, 7, 7, 7, 7, 7, 6)
RUNS = (((2, 6), (2, 5)), ((2, 5), (2, 4)), ((4, 4),), ((4, 4),), ((4, 3),))
BESIDE_FIRST = ((2, 4, SEG), (4, SEG), (SEG,), (SEG,))
TURNS_FIRST = sum(len(b) for b in BESIDE_FIRST)
SECOND_VISITS = 3
PACES = ((STRIPS // 2, 3), (STRIPS // 2, 2))
SB = (N + P - 1) // P
KEYS = W * SB
VISITS = list(FIRST_VISITS) + [k for runs in RUNS for n, k in runs for _ in range(n * SEG)] + [SECOND_VISITS] * NW
VB = (sum(VISITS) + P - 1) // P
EDGE_ROWS = EP // ROW + max(VISITS) * (P // ROW)
PARTS = 3
MASKED = -1048576.0
EXACT = 256.0
EPS = 1e-5
assert NP >= N + P and EP >= E and NCH % SLOTS == 0 and NT % (2 * HT) == 0
assert STRIPS % 2 == 0 and len(VISITS) == 2 * NW and KEYS <= 512 and SB == 12 * SEGS + 1 and SB == 16 * (SEGS - 1) + 1 and STRIP % P == 0
assert SEG % BANKS == 0 and SECOND_VISITS <= UNIT // 2
assert max(k for runs in RUNS for _, k in runs) <= UNIT


def build(nc, t, out):
    with ExitStack() as ctx:
        def sb(name, shape, dt=F32):
            return ctx.enter_context(nc.sbuf_tensor(name, shape, dt))

        def ps(name, shape):
            return ctx.enter_context(nc.psum_tensor(name, shape, F32))

        def sem(name):
            return ctx.enter_context(nc.semaphore(name))

        tables = [nc.dram_tensor(f"table{k}", (NP, D), F32, kind="Internal").ap() for k in range(3)]
        tiles_dram = nc.dram_tensor("tiles", (2, NT), I32, kind="Internal").ap()
        starts_dram = nc.dram_tensor("starts_of_nodes", (NP, 1), I32, kind="Internal").ap()
        own_dram = nc.dram_tensor("own", (P, NP), F32, kind="Internal").ap()
        counts_dram = nc.dram_tensor("counts", (STRIPS, P, SB * STRIP), BF16, kind="Internal").ap()

        consts = sb("consts", [P, 3 * P + KEYS + VB + 2 * SB])
        ident, iota, key_iota = consts[:, 0:P], consts[:, P:2 * P], consts[:, 2 * P:2 * P + KEYS]
        above = consts[:, 2 * P + KEYS:3 * P + KEYS]
        visit_key = consts[:, 3 * P + KEYS:3 * P + KEYS + VB]
        node_half = consts[:, 3 * P + KEYS + VB:3 * P + KEYS + VB + SB]
        minus_node = consts[:, 3 * P + KEYS + VB + SB:]
        iota_bf = sb("iota_bf", [P, P], BF16)
        ones = sb("ones", [P, P])
        zero_strip = sb("zero_strip", [P, STRIP], BF16)
        conv_w = sb("conv_w", [P, 2, D])
        conv_b = sb("conv_b", [P, 2])
        msg_w = sb("msg_w", [P, D])
        msg_b = sb("msg_b", [P, D])
        edge_w = sb("edge_w", [P, TC, D])
        upd_w = sb("upd_w", [P, 2, D])
        upd_b = sb("upd_b", [P, D])
        agg = sb("agg", [P, NP])
        count = sb("count", [P, NB])
        degree = sb("degree", [P, NB])
        dinv = sb("dinv", [P, NB])
        atleast1 = sb("atleast1", [P, NB])
        inv_count = sb("inv_count", [P, NB])
        region_a = sb("region_a", [P, SB * STRIP])
        region_b = sb("region_b", [P, NB * PARTS * D // 2])
        used = [0]

        def carve(columns, dt=F32):
            a = used[0]
            used[0] += columns
            assert used[0] <= SB * STRIP
            return region_a[:, a:a + columns].bitcast(dt)

        dst_i = carve(NT, I32)
        part_i = carve(NT, I32)
        dst_lo = carve(NT // 2, BF16)
        dst_hi = carve(NT // 2, BF16)
        hot_lo = carve(HT * P, BF16).rearrange("p (s t n) -> p s t n", s=2, t=HT)
        hot_hi = carve(HT * NB, BF16).rearrange("p (s t n) -> p s t n", s=2, t=HT)
        tile_min = carve(NT, I32)
        tile_max = carve(NT, I32)
        rows_i = carve(CQ * CE, I32)
        part_columns = region_a[:, VB * 2 * P:VB * 3 * P].bitcast(I32)
        assert VB * 3 * P <= 3 * NT + (HT * (P + NB)) 
        split_edges = region_a[:, 0:VB * 2 * P].rearrange("p (v k e) -> p v k e", v=VB, k=2)
        used[0] = 0
        counts = [carve(SB * STRIP // 2, BF16).rearrange("p (h d) -> p h d", h=SB) for _ in range(2)]
        used[0] = 0
        h2 = carve(NP)
        msgs = carve(2 * TC * D).rearrange("p (s d) -> p s d", s=2)
        attr = carve(SLOTS * P).rearrange("p (s d) -> p s d", s=SLOTS)
        parts = region_b[:].bitcast(BF16).rearrange("p (h k d) -> p h k d", h=NB, k=PARTS)
        visit_edges = region_a[:, VB * 3 * P:VB * 5 * P].bitcast(I32).rearrange("p (v k e) -> p v k e", v=VB, k=2)
        node_tiles = region_b[:, 0:SB * P].rearrange("p (b e) -> p b e", b=SB)
        x1 = region_b[:, 0:NB * D].rearrange("p (b d) -> p b d", d=D)
        dst_rel = sb("dst_rel", [P, NT])
        visit = sb("visit", [P, VB * P, 2])
        visit_now = sb("visit_now", [P, SEG * UNIT, 2])
        visit_plan = sb("visit_plan", [P, 2, VB], I32)
        visit_start = sb("visit_start", [P, VB], I32)
        visit_row = sb("visit_row", [P, VB], I32)
        starts = sb("starts", [P, 3, NB])
        starts_i = sb("starts_i", [NB, P], I32)
        ends_i = sb("ends_i", [SB, P], I32)
        per_node = sb("per_node", [SB, P])
        tile_of = sb("tile_of", [P, SB])
        tile_of_i = sb("tile_of_i", [P, SB], I32)
        below = sb("below", [P, SB])
        mixed_i = sb("mixed_i", [1, 1], I32)
        mixed_f = sb("mixed_f", [1, 1])
        chunk_window = sb("chunk_window", [1, 3, NCH], I32)
        upto = sb("upto", [1, NCH])
        row_min = sb("row_min", [P, CQ * TC], I32)
        row_max = sb("row_max", [P, CQ * TC], I32)
        before_dense = sb("before_dense", [P, 2])
        turns_i = sb("turns_i", [P, 2, 4], I32)
        chunk_base = sb("chunk_base", [P, NCH])
        row_sums = sb("row_sums", [P, 2 * NW])
        found = sb("found", [P, 4])
        judged = sb("judged", [1, 4])
        flag = sb("flag", [1, 2], I32)
        idx = sb("idx", [P, 2, HALF * TC], I32)
        rows = sb("rows", [P, SLOTS, TC * D])
        onehot = sb("onehot", [P, 2, TC, P])
        onehot_x = sb("onehot_x", [P, TC, P])
        iota_x = sb("iota_x", [P, P])
        iota_key = sb("iota_key", [P, KEYS], F16)
        hot_src = sb("hot_src", [P, 2, UNIT, P], BF16)
        hot_key = sb("hot_key", [P, 2, UNIT, KEYS], BF16)
        zero_bf = sb("zero_bf", [P, P], BF16)
        stats = sb("stats", [P, GB, 6])
        moments = sb("moments", [P, GB, 2])
        std = sb("std", [P, GB])
        rstd = sb("rstd", [P, GB])
        eps = sb("eps", [P, 1])
        degree_root = sb("degree_root", [P, NB])
        normed = sb("normed", [P, GB, D])
        feat = sb("feat", [P, GN])
        feat_agg = sb("feat_agg", [P, GN])
        scaled = sb("scaled", [P, GN])
        tab = sb("tab", [P, GB, D])
        rest = [onehot_x[:], onehot[:, 1]]

        def upper(a):
            return a.bitcast(BF16)[:, :, 1::2]

        rows_flat = rows[:].rearrange("p s c -> p (s c)")
        searched_out, greatest = rows_flat[:, 0:NT], rows_flat[:, NT:2 * NT]
        diag = onehot[:, 0]

        ps_sum = [ps("ps_sum0", [P, 512]), ps("ps_sum1", [P, 512])]
        ps_extra = ps("ps_extra", [P, 512])
        ps_pre = [ps("ps_pre0", [P, 512]), ps("ps_pre1", [P, 512])]
        ps_turn = ps("ps_turn", [P, 512])
        ps_node = ps("ps_node", [P, 512])
        ps_feat = ps("ps_feat", [P, 512])

        count_banks = [ps_pre[0], ps_pre[1], ps_turn, ps_extra]

        loaded = sem("loaded")
        setup_ready = sem("setup_ready")
        edge_w_loaded = sem("edge_w_loaded")
        rows_loaded = sem("rows_loaded")
        first_x_loaded = sem("first_x_loaded")
        rows_reduced = sem("rows_reduced")
        tiles_stored = sem("tiles_stored")
        tiles_loaded = sem("tiles_loaded")
        count_copied = sem("count_copied")
        before_ready = sem("before_ready")
        starts_ready = sem("starts_ready")
        mixed_ready = sem("mixed_ready")
        turns_ready = sem("turns_ready")
        searched = sem("searched")
        tiles_found = sem("tiles_found")
        node_tiles_gathered = sem("node_tiles_gathered")
        ends_loaded = sem("ends_loaded")
        per_node_ready = sem("per_node_ready")
        per_node_turned = sem("per_node_turned")
        starts_turned = sem("starts_turned")
        starts_int = sem("starts_int")
        starts_stored = sem("starts_stored")
        starts_gathered = sem("starts_gathered")
        visit_rows_ready = sem("visit_rows_ready")
        visits_gathered = sem("visits_gathered")
        visits_split = sem("visits_split")
        visits_turned = sem("visits_turned")
        visits_copied = sem("visits_copied")
        tables_ready = sem("tables_ready")
        dve_did = sem("dve_did")
        held = {e: sem(f"held_{e}") for e in ("dve", "act", "pool", "sp")}
        parts_split = sem("parts_split")
        lo_ready = sem("lo_ready")
        hi_ready = sem("hi_ready")
        hist_used = sem("hist_used")
        count_ready = sem("count_ready")
        degree_ready = sem("degree_ready")
        root_ready = sem("root_ready")
        G = {k: sem(f"node_{k}") for k in (
            "stats", "moments", "std", "normed", "turned", "diag", "row", "scaled", "shifted", "back", "x1",
            "feat", "products", "tab", "tab_stored", "tab_free", "own_turned", "own", "part", "rest", "h2", "freed")}
        rstd_ready = sem("rstd_ready")
        x_loaded = sem("x_loaded")
        own_stored = sem("own_stored")
        own_restored = [sem("own_restored_0"), sem("own_restored_1")]
        C = {k: sem(f"count_{k}") for k in ("hot", "built", "evacuated", "stored_a", "stored_b", "loaded_a", "loaded_b")}
        applied = [sem("applied_0"), sem("applied_1")]
        strip_added = [sem("strip_added_0"), sem("strip_added_1")]
        most_ready = sem("most_ready")
        most_turned = sem("most_turned")
        flag_ready = sem("flag_ready")
        full_ready = [sem("full_ready_0"), sem("full_ready_1")]
        dense_done = sem("dense_done")

        def gather_sems(name, every=True, apart=HALF):
            gathered = [sem(f"gathered_{s}_{name}") for s in range(SLOTS // apart)]
            return {"every": every, "apart": apart, "gathered": gathered} | {k: sem(f"{k}_{name}") for k in (
                "idx_a", "idx_b", "onehot", "summed", "added",
                "x_onehot", "x_summed", "x_added")}

        shared_passes = [gather_sems(f"shared_{n}", False, 2) for n in range(2)]
        full_passes = [gather_sems(f"full_{n}") for n in range(2)]
        msg_pass = gather_sems("msg", True, 1)
        attr_loaded = [sem("attr_loaded_a"), sem("attr_loaded_b")]
        pre_ready = sem("pre_ready")
        msgs_ready = sem("msgs_ready")
        fin = {k: sem(f"fin_{k}") for k in ("copied", "multiplied", "free", "out", "out_free", "stored", "steps")}

        block = ctx.enter_context(nc.Block())
        N_LOADS = 11
        LAST = NB // GB

        def group(n, g):
            return g + n * NG

        def groups_ahead(engine, step):
            with engine.Fori(0, NG - 1) as g:
                step(g, g + 1)
            step(NG - 1, None)

        def turn_at(first, i):
            return i if isinstance(first, int) else (first + i).with_bounds(min_val=0, max_val=TURNS - 1)

        SEARCHES = [range(q * SB // 4, (q + 1) * SB // 4) for q in range(4)]

        def mixed_of(engine):
            engine.wait_ge(mixed_ready, 1)
            return engine.value_load(mixed_i[0:1, 0:1], min_val=0, max_val=1)

        def units_of(k):
            return [min(UNIT, k - j) for j in range(0, k, UNIT)]

        class At:

            def __init__(self, at, place, ring):
                self.at, self.place, self.ring = at, place % ring, ring

        def hot_slot(unit, u, j):
            place = (unit.place + u) % unit.ring
            return (place, j) if unit.ring == 2 else (place // 2, place % 2 * (UNIT // 2) + j)

        def each_segment(engine, segment, begins, ends):
            unit = 0
            for strip in range(STRIPS):
                begins(strip)
                if strip == 0:
                    for seg in range(SEGS):
                        windows = []
                        for w in range(seg * SEG, seg * SEG + SEG):
                            windows.append((At(w, w, BANKS), At(unit, unit, 2), VISITS[w]))
                            unit += len(units_of(VISITS[w]))
                        segment(strip, seg, windows)
                else:
                    seg0 = 0
                    for n, k in RUNS[strip - 1]:
                        with engine.Fori(0, n) as i:
                            w0, u0 = strip * SW + seg0 * SEG, unit
                            segment(strip, i + seg0, [(At(i * SEG + (w0 + j), w0 + j, BANKS), At(i * SEG + (u0 + j), u0 + j, 2), k)
                                                      for j in range(SEG)])
                        seg0 += n
                        unit += n * SEG
                ends(strip)

        def second_window(u, seg, j):
            at = seg * SEG + j
            units = sum(len(units_of(k)) for k in VISITS[:NW])
            return At(u * SW + (NW + at), at, BANKS), At(u * SW + (units + at), units + at, 4), SECOND_VISITS

        def turn_of(seg, k):
            return sum(len(b) for b in BESIDE_FIRST[:seg]) + k

        def each_pair(engine, pair):
            u0, i0 = 0, 0
            for pairs, pace in PACES:
                with engine.Fori(u0, u0 + pairs) as u:
                    pair(u, u * pace + (i0 - u0 * pace), pace)
                u0 += pairs
                i0 += pairs * pace

        def visits_upto(w):
            return sum(VISITS[:w])

        @block.sync
        def _(sp):
            sp.dma_start(rows_i[0:CR, :], t["dst_rows"].rearrange("r q e -> r (q e)")).then_inc(rows_loaded, 16)
            sp.dma_start(dst_i, t["dst_t"]).then_inc(loaded, 16)
            sp.dma_start(consts[:], t["consts"]).then_inc(loaded, 16)
            sp.dma_start(visit_plan[:], t["visit_plan"]).then_inc(loaded, 16)
            for n in range(2):
                sp.dma_start(conv_w[:, n], t[f"L0_gnn_W{n + 1}"]).then_inc(loaded, 16)
                sp.dma_start(conv_b[:, n:n + 1], t[f"L0_gnn_b{n + 1}"].rearrange("(p a) -> p a", a=1)).then_inc(loaded, 16)
            sp.dma_start(msg_w[:], t["L1_gnn_W1"][0:D, :]).then_inc(loaded, 16)
            sp.dma_start(msg_b[:], t["L1_gnn_b1"].rearrange("(a d) -> a d", a=1).to_broadcast([P, D])).then_inc(loaded, 16)
            sp.dma_start(upd_w[:], t["L1_gnn_W2"].rearrange("(k p) d -> p k d", k=2)).then_inc(loaded, 16)
            sp.dma_start(upd_b[:], t["L1_gnn_b2"].rearrange("(a d) -> a d", a=1).to_broadcast([P, D])).then_inc(loaded, 16)
            sp.wait_ge(rows_reduced, 1)
            sp.dma_start(tiles_dram[0].rearrange("(p q) -> p q", p=CR), row_min[0:CR, :]).then_inc(tiles_stored, 16)
            sp.dma_start(tiles_dram[1].rearrange("(p q) -> p q", p=CR), row_max[0:CR, :]).then_inc(tiles_stored, 16)
            sp.wait_ge(tiles_stored, 32)
            sp.dma_start(tile_min, tiles_dram[0:1, :].to_broadcast([P, NT])).then_inc(tiles_loaded, 16)
            sp.dma_start(tile_max, tiles_dram[1:2, :].to_broadcast([P, NT])).then_inc(tiles_loaded, 16)
            sp.dma_start(agg[:], t["x_nodes"].rearrange("p b d -> p (b d)")).then_inc(first_x_loaded, 16)
            sp.wait_ge(setup_ready, 1)
            for j in range(TC):
                sp.dma_start(edge_w[DE * j:DE * (j + 1), j, :], t["L1_gnn_W1"][D:D + DE, :]).then_inc(edge_w_loaded, 16)
            sp.wait_ge(starts_int, 1)
            sp.dma_start(starts_dram.rearrange("(b p) a -> b (p a)", p=P), starts_i[:]).then_inc(starts_stored, 16)
            mixed = mixed_of(sp)
            with sp.If(mixed < 1):
                sp.wait_ge(starts_stored, 16)
                sp.dma_start(ends_i[:], starts_dram[1:1 + SB * P].rearrange("(b p) a -> b (p a)", p=P)).then_inc(ends_loaded, 16)

            def store_table(n):
                table = tables[n].rearrange("(g b p) d -> g p b d", b=GB, p=P)
                if n == 0:
                    sp.sem_inc(G["tab_free"], 1)
                with sp.Fori(0, NG) as g:
                    sp.wait_ge(G["tab"], group(n, g) + 1)
                    sp.dma_start(table[bass.ds(g, 1)].rearrange("a p b d -> (a p) b d"), tab[:]).then_inc(G["tab_stored"], 16)
                    sp.wait_ge(G["tab_stored"], group(n, g) * 16 + 16)
                    sp.sem_inc(G["tab_free"], 1)

            def load_edges(e, first, turns, messages=False):
                def load_indices(at, h):
                    sp.dma_start(idx[:, h], t["src_t"][:, bass.ds(at * (SLOTS * TC) + h * HALF * TC, HALF * TC)]
                                 ).then_inc(e["idx_" + "ab"[h]], 16)

                for h in range(2):
                    load_indices(turn_at(first, 0), h)
                with sp.Fori(0, turns) as i:
                    for h in range(2):
                        if messages:
                            sp.wait_ge(e["added"], i * SLOTS + HALF * (h + 1))
                            sp.dma_start(attr[:, h * HALF:(h + 1) * HALF],
                                         t["attr_t"][:, bass.ds(turn_at(first, i) * SLOTS + h * HALF, HALF)]
                                         ).then_inc(attr_loaded[h], 16)
                    for h in range(2):
                        for s in range(h * HALF, (h + 1) * HALF, e["apart"]):
                            sp.wait_ge(e["gathered"][s // e["apart"]], (i + 1) * (16 * TC * e["apart"]))
                        load_indices(turn_at(first, i) + 1, h)
                for h in range(2):
                    sp.wait_ge(e["idx_" + "ab"[h]], turns * 16 + 16)
                    sp.sem_inc(held["sp"], 1)

            def shared(n):
                first = sp.value_load(turns_i[0:1, n, 0:1], min_val=0, max_val=TURNS - 1)
                turns = sp.value_load(turns_i[0:1, n, 1:2], min_val=1, max_val=TURNS)
                load_edges(shared_passes[n], first, turns)

            def full(n):
                sp.wait_ge(full_ready[n], 1)
                sp.dma_start(agg[:], own_dram).then_inc(own_restored[n], 16)
                load_edges(full_passes[n], 0, TURNS)

            for n in range(2):
                store_table(n)
                sp.wait_ge(G["own"], NG * (n + 1))
                sp.dma_start(own_dram, agg[:]).then_inc(own_stored, 16)
                if n == 0:
                    sp.wait_ge(turns_ready, 1)
                    shared(n)
                else:
                    with sp.If(flagged < 1):
                        shared(n)
                sp.wait_ge(flag_ready, n + 1)
                flagged = sp.value_load(flag[0:1, n:n + 1], min_val=0, max_val=1)
                with sp.If(flagged > 0):
                    full(n)
            sp.wait_ge(dense_done, 2)
            sp.wait_ge(C["stored_a"], 8 * STRIPS)
            sp.wait_ge(C["stored_b"], 8 * STRIPS)
            sp.dma_start(h2, t["x_nodes"].rearrange("p b d -> p (b d)")).then_inc(x_loaded, 16)
            store_table(2)
            load_edges(msg_pass, 0, TURNS, True)

            rows_out = out.rearrange("(g b p) d -> g p b d", b=GB, p=P)
            sp.sem_inc(fin["out_free"], 1)
            with sp.Fori(0, NG) as g:
                sp.wait_ge(fin["out"], g + 1)
                sp.dma_start(rows_out[bass.ds(g, 1)].rearrange("a p b d -> (a p) b d"), normed[:]).then_inc(fin["stored"], 16)
                sp.wait_ge(fin["stored"], g * 16 + 16)
                sp.sem_inc(fin["out_free"], 1)
            sp.wait_ge(fin["stored"], 16 * NG)

        @block.gpsimd
        def _(pool):
            def gather(e, n, turns):
                with pool.Fori(0, turns) as i:
                    for h in range(2):
                        pool.wait_ge(e["idx_" + "ab"[h]], i * 16 + 16)
                        for k in range(HALF * TC):
                            s, j = h * HALF + k // TC, k % TC
                            if j == 0:
                                pool.wait_ge(e["added"], i * SLOTS + s + 1)
                                pool.sem_inc(held["pool"])
                            nc.gpsimd.indirect_dma_start(
                                rows[:, s, j * D:(j + 1) * D], None, tables[n],
                                bass.IndirectOffsetOnAxis(ap=idx[:, h, k:k + 1], axis=0),
                            ).then_inc(e["gathered"][s // e["apart"]], 16)

            pool.wait_ge(loaded, 16 * N_LOADS)
            mixed = mixed_of(pool)
            with pool.If(mixed < 1):
                tiles = t["dst_rows"].rearrange("r q (t e) -> (r q t) e", e=P)
                for q, blocks in enumerate(SEARCHES):
                    pool.wait_ge(tiles_found, q + 1)
                    for b in blocks:
                        nc.gpsimd.indirect_dma_start(
                            node_tiles[:, b].bitcast(I32), None, tiles,
                            bass.IndirectOffsetOnAxis(ap=tile_of_i[:, b:b + 1], axis=0)).then_inc(node_tiles_gathered, 16)
            pool.wait_ge(starts_stored, 16)
            for b in range(VB):
                nc.gpsimd.indirect_dma_start(
                    visit_start[:, b:b + 1], None, starts_dram,
                    bass.IndirectOffsetOnAxis(ap=visit_plan[:, 0, b:b + 1], axis=0)).then_inc(starts_gathered, 16)
            pool.wait_ge(visit_rows_ready, 1)
            for b in range(VB):
                nc.gpsimd.indirect_dma_start(
                    visit_edges[:, b].rearrange("p k e -> p (k e)"), None, t["edge_rows"],
                    bass.IndirectOffsetOnAxis(ap=visit_row[:, b:b + 1], axis=0)).then_inc(visits_gathered, 16)
            for n in range(2):
                pool.wait_ge(G["tab_stored"], 16 * NG * (n + 1))
                if n == 0:
                    pool.wait_ge(turns_ready, 1)
                    gather(shared_passes[n], n, pool.value_load(turns_i[0:1, n, 1:2], min_val=1, max_val=TURNS))
                else:
                    with pool.If(flagged < 1):
                        gather(shared_passes[n], n, pool.value_load(turns_i[0:1, n, 1:2], min_val=1, max_val=TURNS))
                pool.wait_ge(flag_ready, n + 1)
                flagged = pool.value_load(flag[0:1, n:n + 1], min_val=0, max_val=1)
                with pool.If(flagged > 0):
                    gather(full_passes[n], n, TURNS)
            pool.wait_ge(G["tab_stored"], 16 * NG * 3)
            gather(msg_pass, 2, TURNS)

        @block.tensor
        def _(pe):
            mm = nc.tensor.matmul
            pe.wait_ge(loaded, 16 * N_LOADS)
            pe.wait_ge(setup_ready, 1)
            mixed = mixed_of(pe)
            with pe.If(mixed > 0):
                mm(ps_node[:, 0:NB], zero_bf[:], zero_bf[:, 0:NB], start=True, stop=False, skip_group_check=True)
                pe.sem_inc(hist_used, 2)
                with pe.Fori(0, HSTEPS) as i:
                    for s in range(2):
                        pe.wait_ge(lo_ready, i * 2 + s + 1)
                        pe.wait_ge(hi_ready, i * 2 + s + 1)
                        for j in range(HT):
                            last = mm(ps_node[:, 0:NB], hot_lo[:, s, j], hot_hi[:, s, j], start=False, stop=False,
                                      skip_group_check=True)
                        last.then_inc(hist_used, 1)
                mm(ps_node[:, 0:NB], zero_bf[:], zero_bf[:, 0:NB], start=False, stop=True,
                   skip_group_check=True).then_inc(count_ready, 1)
                pe.wait_ge(count_copied, 1)
                mm(ps_turn[:, 0:NB], above, count[:], start=True, stop=True).then_inc(before_ready, 1)
                mm(ps_feat[:, 0:NB], ones[:], count[:], start=True, stop=True).then_inc(before_ready, 1)
            pe.wait_ge(starts_ready, 1)
            nc.tensor.transpose(ps_sum[0][0:NB, 0:P], starts[:, 0], ident).then_inc(starts_turned, 1)
            with pe.If(mixed < 1):
                pe.wait_ge(per_node_ready, 1)
                nc.tensor.transpose(ps_sum[1][:, 0:SB], per_node[:], ident[0:SB, 0:SB]).then_inc(per_node_turned, 1)

            def turn(to, of):
                for b in range(GB):
                    last = nc.tensor.transpose(to[:, b * P:(b + 1) * P], of(b), ident)
                return last

            def node_phase(n):
                def row(g):
                    pe.wait_ge(G["diag"], group(n, g) - NG + 1)
                    mm(ps_pre[1][:], ones[:], diag.rearrange("p b n -> p (b n)"), start=True, stop=True).then_inc(G["row"], 1)

                def back(g):
                    pe.wait_ge(G["shifted"], g + 1)
                    turn(ps_pre[0], lambda b: feat_agg[:, b * P:(b + 1) * P]).then_inc(G["back"], 1)

                def turned(g):
                    pe.wait_ge(G["normed"], g + 1 + NG * (n // 2))
                    turn(ps_turn, lambda b: normed[:, b]).then_inc(G["turned"], 1)

                def step(g, ahead):
                    k = group(n, g)
                    if n == 2:
                        if ahead is not None:
                            row(ahead)
                            back(ahead)
                        turned(g)
                    pe.wait_ge(G["feat"], k + 1)
                    pe.wait_ge(G["freed"], k + 1)
                    w = conv_w[:, n] if n < 2 else msg_w[:]
                    for b in range(GB):
                        last = mm(ps_node[:, b * D:(b + 1) * D], feat[:, b * P:(b + 1) * P], w, start=True, stop=True)
                    last.then_inc(G["products"], 1)
                    if n == 1 and ahead is not None:
                        row(ahead)
                    if n < 2:
                        pe.wait_ge(G["tab"], k + 1)
                        turn(ps_feat, lambda b: tab[:, b]).then_inc(G["own_turned"], 1)
                    if n == 0 and ahead is not None:
                        turned(ahead)

                if n:
                    row(0)
                if n == 2:
                    back(0)
                if n == 0:
                    turned(0)
                groups_ahead(pe, step)

            def sum_chunk(e, i, s, lhs):
                c = i * SLOTS + s
                if e["every"]:
                    more = pe.value_load(chunk_window[0:1, 1, bass.ds(c, 1)], min_val=0, max_val=NB)
                    with pe.If(more > 0):
                        a = pe.value_load(chunk_window[0:1, 2, bass.ds(c, 1)], min_val=0, max_val=NCH * NB)
                        with pe.Fori(0, more) as k:
                            pe.wait_ge(e["x_onehot"], a + k + 2)
                            pe.wait_ge(e["x_added"], a + k + 1)
                            for j in range(TC):
                                last = mm(ps_extra[:, 0:P], lhs[:, j * D:(j + 1) * D], onehot_x[:, j], start=(j == 0), stop=(j == TC - 1))
                            last.then_inc(e["x_summed"], 1)
                pe.wait_ge(e["added"], c + 7)
                pe.wait_ge(e["onehot"], c + 1)
                for j in range(TC):
                    last = mm(ps_sum[s % 2][:, 0:P], lhs[:, j * D:(j + 1) * D], onehot[:, s % 2, j], start=(j == 0), stop=(j == TC - 1))
                last.then_inc(e["summed"], 1)

            def edge_turn(e, i, messages=False, between=lambda s: None):
                def before(s):
                    if s % e["apart"] == 0:
                        pe.wait_ge(e["gathered"][s // e["apart"]], (i + 1) * (16 * TC * e["apart"]))
                    if messages:
                        if s % HALF == 0:
                            pe.wait_ge(attr_loaded[s // HALF], i * 16 + 16)
                        pe.wait_ge(msgs_ready, i * SLOTS + s + 1)
                        mm(ps_pre[s % 2][:], attr[:, s], edge_w[:].rearrange("p j d -> p (j d)"), start=True, stop=False)
                        mm(ps_pre[s % 2][:], ident, rows[:, s], start=False, stop=True).then_inc(pre_ready, 1)

                def after(s):
                    if messages:
                        pe.wait_ge(msgs_ready, i * SLOTS + s + 3)
                    sum_chunk(e, i, s, msgs[:, s % 2] if messages else rows[:, s])

                before(0)
                for s in range(1, SLOTS):
                    between(s - 1)
                    before(s)
                    after(s - 1)
                between(SLOTS - 1)
                after(SLOTS - 1)

            def build_window(w, unit, k):
                bank = count_banks[w.place][:, 0:KEYS]
                pe.wait_ge(C["evacuated"], w.at + 1)
                for u, n in enumerate(units_of(k)):
                    pe.wait_ge(C["hot"], unit.at + (u + 1))
                    for j in range(n):
                        place, slot = hot_slot(unit, u, j)
                        ins = mm(bank, hot_src[:, place, slot], hot_key[:, place, slot], start=(u == 0 and j == 0),
                                 stop=(u * UNIT + j == k - 1), skip_group_check=True)
                    ins.then_inc(C["built"], 1)

            def strip_bank(buf):
                return (ps_feat if buf else ps_node)[:, 0:STRIP]

            def apply(buf, h, first=False, last=False):
                for k in range(PARTS):
                    ins = mm(strip_bank(buf), parts_at(h, k), counts_at(buf, h), start=first and k == 0,
                             stop=last and k == PARTS - 1, skip_group_check=True)
                return ins

            def parts_at(h, k):
                if isinstance(h, int):
                    return parts[:, h, k]
                return parts[:, bass.ds(h, 1), k].rearrange("p a d -> p (a d)")

            def counts_at(buf, h):
                if isinstance(h, int):
                    return counts[buf][:, h]
                return counts[buf][:, bass.ds(h, 1)].rearrange("p a d -> p (a d)")

            def shared(n):
                e = shared_passes[n]
                turns = pe.value_load(turns_i[0:1, n, 1:2], min_val=1, max_val=TURNS)
                pe.sem_inc(e["summed"], 2)
                pe.wait_ge(G["part"], NG * PARTS * (n + 1))

                def turn_beside(i):
                    with pe.If(turns > i):
                        edge_turn(e, i)

                if n == 0:
                    pe.sem_inc(C["built"], 2)

                    def segment(strip, seg, windows):
                        other = 1 - strip % 2
                        for j, (w, unit, k) in enumerate(windows):
                            build_window(w, unit, k)
                            if strip == 0 and j + 1 in BESIDE_FIRST[seg]:
                                turn_beside(turn_of(seg, BESIDE_FIRST[seg].index(j + 1)))
                            if strip:
                                for h in (j + j // 2, ) if j % 2 else (j + j // 2, j + j // 2 + 1):
                                    apply(other, seg * 12 + h + (j % 2))
                        if strip:
                            turn_beside(seg + ((strip - 1) * SEGS + TURNS_FIRST))

                    def strip_begins(strip):
                        if strip:
                            pe.wait_ge(C["evacuated"], strip * SW + BANKS)
                            pe.wait_ge(strip_added[1 - strip % 2], (strip + 1) // 2)
                            apply(1 - strip % 2, SB - 1, first=True)

                    def strip_ends(strip):
                        if strip:
                            mm(strip_bank(1 - strip % 2), zero_bf[:], zero_strip[:], start=False, stop=True,
                               skip_group_check=True).then_inc(applied[1 - strip % 2], 1)

                    each_segment(pe, segment, strip_begins, strip_ends)
                    pe.wait_ge(C["evacuated"], NW + BANKS)
                    pe.wait_ge(strip_added[1], STRIPS // 2)
                    for h in range(SB):
                        ins = apply(1, h, first=(h == 0), last=(h == SB - 1))
                    ins.then_inc(applied[1], 1)
                else:
                    def pair(u, turn0, pace):
                        for seg in range(SEGS):
                            if seg == 1:
                                pe.wait_ge(C["loaded_b"], u * 16 + 16)
                                pe.wait_ge(strip_added[1], u + (STRIPS // 2 + 1))
                                apply(1, SB - 1, first=True)
                            for j in range(SEG):
                                build_window(*second_window(u, seg, j))
                                if seg:
                                    for h in range(2):
                                        apply(1, (seg - 1) * 16 + j * 2 + h)
                            if seg % 2:
                                turn_beside(turn0 + seg // 2)
                        mm(strip_bank(1), zero_bf[:], zero_strip[:], start=False, stop=True,
                           skip_group_check=True).then_inc(applied[1], 1)
                        pe.wait_ge(C["evacuated"], u * SW + (NW + SW + BANKS))
                        pe.wait_ge(strip_added[0], u + (STRIPS // 2 + 1))

                        def apply_some(s):
                            for h in range(s * SB // SLOTS, (s + 1) * SB // SLOTS):
                                ins = apply(0, h, first=(h == 0), last=(h == SB - 1))
                            if s == SLOTS - 1:
                                ins.then_inc(applied[0], 1)

                        def apply_alone():
                            for s in range(SLOTS):
                                apply_some(s)

                        if pace > 2:
                            with pe.If(turns > turn0 + 2):
                                edge_turn(e, turn0 + 2, between=apply_some)
                            with pe.Else():
                                apply_alone()
                        else:
                            apply_alone()

                    each_pair(pe, pair)
                beside = sum(n * pace for n, pace in PACES) if n else (STRIPS - 1) * SEGS + TURNS_FIRST
                with pe.If(turns > beside):
                    with pe.Fori(beside, turns) as i:
                        edge_turn(e, i)
                pe.nop()

            def full(n):
                pe.sem_inc(full_passes[n]["summed"], 2)
                with pe.Fori(0, TURNS) as i:
                    edge_turn(full_passes[n], i)

            node_phase(0)
            pe.wait_ge(visits_split, 1)
            for b in range(VB):
                if b >= 2:
                    pe.wait_ge(visits_copied, b - 1)
                for k in range(2):
                    last = nc.tensor.transpose(ps_sum[b % 2][:, k * P:(k + 1) * P], split_edges[:, b, k], ident)
                last.then_inc(visits_turned, 1)
            pe.wait_ge(tables_ready, 1)
            shared(0)

            def verdict(n):
                pe.wait_ge(most_ready, n + 1)
                mm(ps_turn[0:1, 0:P], found[:, 0:1], ident, start=True, stop=True).then_inc(most_turned, 1)
                mm(ps_extra[0:1, 0:1], found[:, 3:4], ones[:, 0:1], start=True, stop=True).then_inc(most_turned, 1)
                pe.wait_ge(flag_ready, n + 1)
                flagged = pe.value_load(flag[0:1, n:n + 1], min_val=0, max_val=1)
                with pe.If(flagged > 0):
                    full(n)
                return flagged

            flagged = verdict(0)
            node_phase(1)
            with pe.If(flagged < 1):
                shared(1)
            verdict(1)
            node_phase(2)
            pe.sem_inc(msg_pass["summed"], 2)
            pe.wait_ge(edge_w_loaded, 16 * TC)
            with pe.Fori(0, TURNS) as i:
                edge_turn(msg_pass, i, True)

            pe.sem_inc(fin["multiplied"], 1)
            with pe.Fori(0, NG) as g:
                pe.wait_ge(fin["copied"], g * 2 + 2)
                pe.wait_ge(fin["free"], g + 1)
                for b in range(GB):
                    mm(ps_node[:, b * D:(b + 1) * D], feat[:, b * P:(b + 1) * P], upd_w[:, 0], start=True, stop=True)
                for b in range(GB):
                    last = mm(ps_feat[:, b * D:(b + 1) * D], feat_agg[:, b * P:(b + 1) * P], upd_w[:, 1], start=True, stop=True)
                last.then_inc(fin["multiplied"], 1)

        @block.scalar
        def _(act):
            def hold(s, value):
                act.wait_ge(s, value)
                act.sem_inc(held["act"], 1)

            mixed = mixed_of(act)
            with act.If(mixed < 1):
                for b in range(SB):
                    if b:
                        act.wait_ge(searched, b)
                    nc.scalar.activation(searched_out, greatest, ACT.Sign, bias=minus_node[:, b:b + 1],
                                         accum_out=below[:, b:b + 1]).then_inc(searched, 1)
            act.wait_ge(degree_ready, 1)
            nc.scalar.activation(degree_root[:], degree[:], ACT.Sqrt).then_inc(root_ready, 1)

            def node_phase(n):
                def std_of(g):
                    act.wait_ge(G["moments"], g + 1 + NG * (n // 2))
                    nc.scalar.activation(std[:], moments[:, :, 1], ACT.Sqrt, bias=eps[:]).then_inc(G["std"], 1)

                def shifted(g):
                    act.wait_ge(G["scaled"], NG + g + 1)
                    nc.scalar.activation(feat_agg[:], scaled[:], ACT.Identity, bias=conv_b[:, 1:2]).then_inc(G["shifted"], 1)

                def features(g):
                    if n == 1:
                        act.wait_ge(G["scaled"], g + 1)
                    else:
                        act.wait_ge(G["turned"], g + 1 + NG * (n // 2))
                    act.wait_ge(G["freed"], group(n, g) + 1)
                    if n == 1:
                        nc.scalar.activation(feat[:], scaled[:], ACT.Relu, bias=conv_b[:, 0:1]).then_inc(G["feat"], 1)
                    else:
                        nc.scalar.activation(feat[:], ps_turn[:], ACT.Relu).then_inc(G["feat"], 1)
                    if n == 2:
                        nc.scalar.activation(h2[:, bass.ds(g * GN, GN)], ps_turn[:], ACT.Relu).then_inc(G["h2"], 1)

                def step(g, ahead):
                    k = group(n, g)
                    blocks = bass.ds(g * GB, GB)
                    if n == 2:
                        std_of(g)
                        if ahead is not None:
                            shifted(ahead)
                        features(g)
                        return
                    if n == 0 and ahead is not None:
                        std_of(ahead)
                    hold(G["tab"], k + 1)
                    nc.scalar.activation(parts[:, blocks, 0], upper(tab[:]), ACT.Copy).then_inc(G["part"], 1)
                    hold(G["own_turned"], k + 1)
                    nc.scalar.activation(agg[:, bass.ds(g * GN, GN)], ps_feat[:], ACT.Copy).then_inc(G["own"], 1)
                    for j in range(1, PARTS):
                        hold(G["rest"], k * 2 + j)
                        nc.scalar.activation(parts[:, blocks, j], upper(rest[0]) if j == 1 else rest[1], ACT.Copy).then_inc(G["part"], 1)
                        if j == 1 and ahead is not None:
                            features(ahead)

                if n == 0:
                    std_of(0)
                if n == 2:
                    shifted(0)
                else:
                    features(0)
                groups_ahead(act, step)

            def segment(strip, seg, windows):
                for j, (w, unit, k) in enumerate(windows):
                    hold(C["built"], unit.at + (len(units_of(k)) + 2))
                    nc.scalar.activation(
                        counts[strip % 2][:, :, bass.ds(seg * (SEG * W) + j * W, W)],
                        count_banks[w.place][:, 0:KEYS].rearrange("p (d h) -> p h d", h=SB), ACT.Copy,
                        accum_out=row_sums[:, bass.ds(w.at, 1)]).then_inc(C["evacuated"], 1)

            def strip_begins(strip):
                if strip >= 2:
                    free_counts(strip % 2, strip // 2)

            def strip_ends(strip):
                act.wait_ge(C["evacuated"], strip * SW + (SW + BANKS))
                act.dma_start(counts_dram[strip], counts[strip % 2].rearrange("p h d -> p (h d)")
                              ).then_inc(C["stored_" + "ab"[strip % 2]], 16)

            def strip_dram(strip):
                return counts_dram[bass.ds(strip, 1)].rearrange("a p c -> (a p) c")

            def free_counts(buf, uses):
                act.wait_ge(applied[buf], uses)
                act.wait_ge(C["stored_" + "ab"[buf]], uses * 16)
                act.sem_inc(held["act"], 1)

            def shared(n):
                if n == 0:
                    act.sem_inc(C["evacuated"], BANKS)
                    each_segment(act, segment, strip_begins, strip_ends)
                else:
                    act.wait_ge(C["stored_a"], 8 * STRIPS)
                    act.wait_ge(C["stored_b"], 8 * STRIPS)
                    act.wait_ge(applied[1], STRIPS // 2)
                    act.dma_start(counts[1].rearrange("p h d -> p (h d)"), counts_dram[0]).then_inc(C["loaded_b"], 16)
                    with act.Fori(0, STRIPS) as u:
                        act.wait_ge(applied[0], u + STRIPS // 2)
                        act.sem_inc(held["act"], 1)
                        for seg in range(SEGS):
                            segment(STRIPS, seg, [second_window(u, seg, j) for j in range(SEG)])
                        with act.If(u < STRIPS - 1):
                            act.wait_ge(applied[1], u + (STRIPS // 2 + 1))
                            act.dma_start(counts[1].rearrange("p h d -> p (h d)"), strip_dram((u + 1).with_bounds(min_val=1, max_val=STRIPS - 1))).then_inc(C["loaded_b"], 16)

            node_phase(0)
            shared(0)
            act.wait_ge(flag_ready, 1)
            flagged = act.value_load(flag[0:1, 0:1], min_val=0, max_val=1)
            node_phase(1)
            with act.If(flagged < 1):
                shared(1)
            act.wait_ge(x_loaded, 16)
            node_phase(2)
            act.wait_ge(G["h2"], NG)
            e = msg_pass
            act.sem_inc(msgs_ready, 2)
            with act.Fori(0, TURNS) as i:
                for s in range(SLOTS):
                    act.wait_ge(pre_ready, i * SLOTS + s + 1)
                    act.wait_ge(e["summed"], i * SLOTS + s + 1)
                    nc.scalar.activation(msgs[:, s % 2], ps_pre[s % 2][:], ACT.Relu).then_inc(msgs_ready, 1)
            act.wait_ge(e["added"], SLOTS + NCH)
            with act.Fori(0, NG) as g:
                hold(fin["multiplied"], g + 1)
                nc.scalar.activation(feat[:], h2[:, bass.ds(g * GN, GN)], ACT.Copy).then_inc(fin["copied"], 1)
                nc.scalar.activation(feat_agg[:], agg[:, bass.ds(g * GN, GN)], ACT.Copy).then_inc(fin["copied"], 1)

        @block.vector
        def _(dve):
            v = nc.vector
            steps = [0]

            def link(ins):
                steps[0] += 1
                ins.then_inc(dve_did, 1)
                dve.wait_ge(dve_did, steps[0])

            def hold(s, value):
                dve.wait_ge(s, value)
                dve.sem_inc(held["dve"], 1)

            v.memset(edge_w[:], 0.0).then_inc(dve_did, 1)
            v.memset(row_sums[:], 0.0).then_inc(dve_did, 1)
            v.memset(ones[:], 1.0).then_inc(dve_did, 1)
            v.memset(zero_bf[:], 0.0).then_inc(dve_did, 1)
            v.memset(zero_strip[:], 0.0).then_inc(dve_did, 1)
            steps[0] = 5
            link(v.memset(eps[:], EPS))
            dve.sem_inc(setup_ready, 1)
            dve.wait_ge(rows_loaded, 16)
            row = rows_i[0:CR, :].rearrange("p (t e) -> p t e", e=P)
            v.tensor_reduce(row_min[0:CR, :], row, AX.X, ALU.min)
            link(v.tensor_reduce(row_max[0:CR, :], row, AX.X, ALU.max))
            dve.drain()
            dve.sem_inc(rows_reduced, 1)
            dve.wait_ge(loaded, 16 * N_LOADS)
            v.tensor_copy(iota_bf[:], iota)
            v.tensor_copy(iota_key[:], key_iota)
            dve.wait_ge(tiles_loaded, 32)
            v.tensor_copy(greatest, tile_max)
            link(v.tensor_tensor(searched_out[0:1, 0:NT - 1], tile_max[0:1, 0:NT - 1], tile_min[0:1, 1:NT], ALU.is_gt))
            link(v.tensor_reduce(mixed_f[:], searched_out[0:1, 0:NT - 1], AX.X, ALU.max))
            link(v.tensor_copy(mixed_i[:], mixed_f[:]))
            dve.sem_inc(mixed_ready, 1)
            dve.wait_ge(tiles_loaded, 32)
            by_chunk = [a.rearrange("p (c t) -> p c t", t=TC) for a in (tile_min, tile_max, dst_i, dst_rel[:])]
            chunk_min = part_i[:, 0:NCH]
            chunk_max = part_i[:, NCH:2 * NCH]
            link(v.tensor_reduce(chunk_min, by_chunk[0], AX.X, ALU.min))
            link(v.tensor_reduce(chunk_max, by_chunk[1], AX.X, ALU.max))
            link(v.tensor_tensor(by_chunk[3], by_chunk[2], chunk_min.unsqueeze(2).to_broadcast([P, NCH, TC]), ALU.subtract))
            before = part_i[:].bitcast(F32)
            link(v.tensor_copy(chunk_window[:, 0], chunk_min[0:1]))
            link(v.tensor_tensor(chunk_max[0:1], chunk_max[0:1], chunk_min[0:1], ALU.subtract))
            link(v.tensor_single_scalar(chunk_window[:, 1], chunk_max[0:1], 7, ALU.arith_shift_right))

            def counted_ahead(table, f):
                link(v.tensor_copy(f, table[:, 1]))
                link(v.tensor_tensor_scan(f, f, f, 0.0, ALU.add, ALU.bypass))
                link(v.tensor_tensor(table[:, 2], f, table[:, 1], ALU.subtract))

            counted_ahead(chunk_window, upto[:])
            link(v.tensor_copy(chunk_base[:], chunk_min))
            link(v.tensor_scalar(before, dst_i, float(STRIPS * STRIP), MASKED, ALU.is_lt, ALU.mult))
            link(v.tensor_tensor(dst_rel[:], dst_rel[:], before, ALU.add))
            far = tile_max.bitcast(F32)
            link(v.tensor_copy(far, tile_max))
            link(v.tensor_tensor_scan(far, far, far, -1.0, ALU.max, ALU.bypass))
            for n in range(2):
                link(v.tensor_scalar(before, far, float(IN_COUNTS[n] * STRIP), None, ALU.is_lt))
                link(v.tensor_reduce(before_dense[:, 0:1], before, AX.X, ALU.add))
                link(v.tensor_copy(turns_i[:, n, 2:3], before_dense[:, 0:1]))
                link(v.tensor_single_scalar(turns_i[:, n, 3:4], turns_i[:, n, 2:3], 5, ALU.arith_shift_right))
                link(v.tensor_copy(before_dense[:, 1:2], turns_i[:, n, 3:4]))
                link(v.tensor_scalar(before_dense[:, 0:1], before_dense[:, 1:2], float(TURNS - 1), None, ALU.min))
                link(v.tensor_copy(turns_i[:, n, 0:1], before_dense[:, 0:1]))
                link(v.tensor_scalar(before_dense[:, 1:2], before_dense[:, 0:1], -1.0, float(TURNS), ALU.mult, ALU.add))
                link(v.tensor_copy(turns_i[:, n, 1:2], before_dense[:, 1:2]))
            dve.sem_inc(turns_ready, 1)
            mixed = mixed_of(dve)
            with dve.If(mixed > 0):
                v.tensor_single_scalar(part_i, dst_i, P - 1, ALU.bitwise_and)
                dve.drain()
                v.tensor_copy(dst_lo, part_i)
                dve.drain()
                v.tensor_single_scalar(part_i, dst_i, 7, ALU.arith_shift_right)
                dve.drain()
                v.tensor_copy(dst_hi, part_i).then_inc(parts_split, 1)
                dve.wait_ge(parts_split, 1)
                with dve.Fori(0, HSTEPS) as i:
                    for s in range(2):
                        dve.wait_ge(hist_used, i * 2 + s + 1)
                        for hot, of, n, ready in ((hot_lo, dst_lo, P, lo_ready), (hot_hi, dst_hi, NB, hi_ready)):
                            v.tensor_tensor(hot[:, s], iota_bf[:, None, 0:n].to_broadcast([P, HT, n]),
                                            of[:, bass.ds(i * (2 * HT) + s * HT, HT)].unsqueeze(2).to_broadcast([P, HT, n]),
                                            ALU.is_equal).then_inc(ready, 1)
                dve.wait_ge(count_ready, 1)
                v.tensor_copy(count[:], ps_node[:, 0:NB])
                dve.drain()
                dve.sem_inc(count_copied, 1)
                dve.wait_ge(before_ready, 2)
                v.tensor_copy(starts[:, 1], ps_feat[:, 0:NB])
                dve.drain()
                v.tensor_tensor_scan(starts[:, 2], starts[:, 1], starts[:, 1], 0.0, ALU.add, ALU.bypass)
                dve.drain()
                v.tensor_tensor(starts[:, 2], starts[:, 2], starts[:, 1], ALU.subtract)
                dve.drain()
                v.tensor_tensor(starts[:, 0], starts[:, 2], ps_turn[:, 0:NB], ALU.add).then_inc(starts_ready, 1)
            with dve.Else():
                for q, blocks in enumerate(SEARCHES):
                    at = slice(blocks[0], blocks[-1] + 1)
                    dve.wait_ge(searched, blocks[-1] + 1)
                    v.tensor_scalar(tile_of[:, at], below[:, at], -0.5, NT / 2, ALU.mult, ALU.add)
                    dve.drain()
                    v.tensor_scalar(tile_of[:, at], tile_of[:, at], float(NT - 1), None, ALU.min)
                    dve.drain()
                    v.tensor_copy(tile_of_i[:, at], tile_of[:, at])
                    dve.drain()
                    dve.sem_inc(tiles_found, 1)
                v.memset(starts[:, 0, SB:], float(EP))
                v.tensor_scalar(starts[:, 1, 0:SB], tile_of[:], float(P), None, ALU.mult)
                dve.wait_ge(node_tiles_gathered, 16 * SB)
                v.tensor_tensor(node_tiles, node_tiles.bitcast(I32), node_half.unsqueeze(2).to_broadcast([P, SB, P]), ALU.is_lt)
                dve.drain()
                v.tensor_reduce(starts[:, 2, 0:SB], node_tiles, AX.X, ALU.add)
                dve.drain()
                v.tensor_tensor(starts[:, 0, 0:SB], starts[:, 1, 0:SB], starts[:, 2, 0:SB], ALU.add).then_inc(starts_ready, 1)
            dve.wait_ge(starts_turned, 1)
            v.tensor_copy(starts_i[:], ps_sum[0][0:NB, 0:P]).then_inc(starts_int, 1)
            with dve.If(mixed < 1):
                dve.wait_ge(starts_int, 1)
                dve.wait_ge(ends_loaded, 16)
                v.tensor_tensor(per_node[:], ends_i[:], starts_i[0:SB, :], ALU.subtract).then_inc(per_node_ready, 1)
                v.memset(count[:, SB:], 0.0)
                dve.wait_ge(per_node_turned, 1)
                v.tensor_copy(count[:, 0:SB], ps_sum[1][:, 0:SB])
                dve.drain()
            v.tensor_scalar(degree[:], count[:], 1.0, None, ALU.add).then_inc(degree_ready, 1)
            link(v.tensor_scalar(atleast1[:], count[:], 1.0, None, ALU.max))
            link(v.reciprocal(inv_count[:], atleast1[:]))
            dve.wait_ge(root_ready, 1)
            link(v.reciprocal(dinv[:], degree_root[:]))
            dve.wait_ge(starts_gathered, 16 * VB)
            link(v.tensor_single_scalar(visit_start[:], visit_start[:], 4, ALU.arith_shift_right))
            v.tensor_tensor(visit_row[:], visit_start[:], visit_plan[:, 1], ALU.add).then_inc(visit_rows_ready, 1)

            def block_of(a, g):
                return lambda b: a[:, bass.ds(g * GN + b * P, P)]

            def mean_and_variance(block_of, n, g):
                k = g + NG * (n // 2)
                for b in range(GB):
                    v.bn_stats(stats[:, b], block_of(b)).then_inc(G["stats"], 1)
                if not (isinstance(k, int) and k == 0):
                    hold(G["normed"], k)
                hold(G["stats"], k * GB + GB)
                for b in range(GB):
                    last = v.bn_aggr(moments[:, b], stats[:, b])
                last.then_inc(G["moments"], 1)

            def normalise(block_of, n, g):
                k = g + NG * (n // 2)
                dve.wait_ge(G["moments"], k + 1)
                dve.wait_ge(G["std"], k + 1)
                v.reciprocal(rstd[:], std[:]).then_inc(rstd_ready, 1)
                dve.wait_ge(rstd_ready, k + 1)
                for b in range(GB):
                    last = v.tensor_scalar(normed[:, b], block_of(b), moments[:, b, 0:1], rstd[:, b:b + 1],
                                           ALU.subtract, ALU.mult)
                last.then_inc(G["normed"], 1)

            def node_phase(n):
                def dinv_of(g):
                    return dinv[:, bass.ds(g * GB, GB)].unsqueeze(2)

                def diagonal(g):
                    v.tensor_tensor(diag, ident[:, None, :].to_broadcast([P, GB, P]), dinv_of(g).to_broadcast([P, GB, P]),
                                    ALU.mult).then_inc(G["diag"], 1)

                def scale(g):
                    dve.wait_ge(G["row"], group(n, g) - NG + 1)
                    v.tensor_tensor(scaled[:], agg[:, bass.ds(g * GN, GN)], ps_pre[1][:], ALU.mult).then_inc(G["scaled"], 1)

                def add_x(g):
                    cols = bass.ds(g * GN, GN)
                    dve.wait_ge(G["back"], g + 1)
                    v.tensor_tensor(region_b[:, cols], h2[:, cols], ps_pre[0][:], ALU.add).then_inc(G["x1"], 1)

                def rows_of(g):
                    k = group(n, g)
                    nodes = ps_node[:].rearrange("p (b d) -> p b d", b=GB)
                    dve.wait_ge(G["products"], k + 1)
                    dve.wait_ge(G["tab_free"], k + 1)
                    if n < 2:
                        v.tensor_tensor(tab[:], nodes, dinv_of(g).to_broadcast([P, GB, D]), ALU.mult).then_inc(G["tab"], 1)
                    else:
                        v.tensor_tensor(tab[:], nodes, msg_b[:, None, :].to_broadcast([P, GB, D]), ALU.add).then_inc(G["tab"], 1)
                    dve.wait_ge(G["tab"], k + 1)
                    if n == 2:
                        dve.wait_ge(G["h2"], g + 1)
                    dve.sem_inc(G["freed"], 1)

                def step_0_or_1(g, ahead):
                    k = group(n, g)
                    if ahead is not None:
                        if n == 0:
                            mean_and_variance(block_of(agg, ahead), n, ahead)
                        else:
                            diagonal(ahead)
                    rows_of(g)
                    if ahead is not None:
                        if n == 0:
                            normalise(block_of(agg, ahead), n, ahead)
                        else:
                            scale(ahead)
                    for j in range(PARTS - 1):
                        whole = rest[0] if j else tab[:]
                        v.tensor_tensor(rest[j], whole, upper(whole), ALU.subtract).then_inc(G["rest"], 1)
                        dve.wait_ge(G["rest"], k * 2 + j + 1)
                    dve.wait_ge(G["own"], k + 1)
                    dve.wait_ge(G["part"], k * PARTS + PARTS)

                def step_2(g, ahead):
                    if ahead is not None:
                        diagonal(ahead)
                    hold(G["x1"], g + 1)
                    mean_and_variance(block_of(region_b, g), n, g)
                    if ahead is not None:
                        scale(ahead)
                    normalise(block_of(region_b, g), n, g)
                    if ahead is not None:
                        add_x(ahead)
                    rows_of(g)

                if n == 0:
                    dve.wait_ge(first_x_loaded, 16)
                    dve.sem_inc(G["freed"], 1)
                    mean_and_variance(block_of(agg, 0), n, 0)
                    normalise(block_of(agg, 0), n, 0)
                else:
                    diagonal(0)
                    scale(0)
                if n == 2:
                    add_x(0)
                groups_ahead(dve, step_2 if n == 2 else step_0_or_1)

            def edge_turn(e, i, first):
                bases = [None] * SLOTS
                if not e["every"]:
                    _, bases = nc.values_load_multi_w_load_instructions(
                        chunk_window[0:1, 0, bass.ds(turn_at(first, i) * SLOTS, SLOTS)], engines=[mybir.EngineType.DVE],
                        min_val=0, max_val=NP - P)

                def hot(s):
                    at = turn_at(first, i) * SLOTS + s
                    if e["every"]:
                        bases[s] = dve.value_load(chunk_window[0:1, 0, bass.ds(at, 1)], min_val=0, max_val=NP - P)
                    v.tensor_tensor(onehot[:, s % 2], iota[:, None, :].to_broadcast([P, TC, P]),
                                    dst_rel[:, bass.ds(at * TC, TC)].unsqueeze(2).to_broadcast([P, TC, P]),
                                    ALU.is_equal).then_inc(e["onehot"], 1)

                def add(s):
                    c = i * SLOTS + s
                    at = turn_at(first, i) * SLOTS + s
                    if e["every"]:
                        more = dve.value_load(chunk_window[0:1, 1, bass.ds(at, 1)], min_val=0, max_val=NB)
                        with dve.If(more > 0):
                            a = dve.value_load(chunk_window[0:1, 2, bass.ds(at, 1)], min_val=0, max_val=NCH * NB)
                            v.tensor_copy(iota_x[:], iota)
                            dve.drain()
                            with dve.Fori(0, more) as k:
                                v.tensor_scalar(iota_x[:], iota_x[:], float(P), None, ALU.add)
                                dve.drain()
                                v.tensor_tensor(onehot_x[:], iota_x[:, None, :].to_broadcast([P, TC, P]),
                                                dst_rel[:, bass.ds(at * TC, TC)].unsqueeze(2).to_broadcast([P, TC, P]),
                                                ALU.is_equal).then_inc(e["x_onehot"], 1)
                                dve.wait_ge(e["x_summed"], a + k + 1)
                                w = agg[:, bass.ds((bases[s] + k * P + P).with_bounds(min_val=0, max_val=NP - P), P)]
                                v.tensor_tensor(w, w, ps_extra[:, 0:P], ALU.add).then_inc(e["x_added"], 1)
                                dve.drain()
                    dve.wait_ge(e["summed"], c + 3)
                    dve.wait_ge(e["added"], c + SLOTS)
                    w = agg[:, bass.ds(bases[s], P)]
                    v.tensor_tensor(w, w, ps_sum[s % 2][:, 0:P], ALU.add).then_inc(e["added"], 1)

                hot(0)
                for s in range(1, SLOTS):
                    hot(s)
                    add(s - 1)
                add(SLOTS - 1)

            def start_pass(e):
                dve.sem_inc(e["added"], SLOTS)
                dve.sem_inc(e["x_added"], 1)
                dve.sem_inc(e["x_onehot"], 1)

            def one_hots(now, windows):
                at = 0
                for w, unit, k in windows:
                    for u, n in enumerate(units_of(k)):
                        hold(C["built"], unit.at + (u + 3 - unit.ring))
                        for j in range(n):
                            place, slot = hot_slot(unit, u, j)
                            v.tensor_scalar(hot_src[:, place, slot], iota_bf[:], now[:, at, 0:1], None, ALU.is_equal)
                            ins = v.tensor_scalar(hot_key[:, place, slot], iota_key[:], now[:, at, 1:2], None, ALU.is_equal)
                            at += 1
                        ins.then_inc(C["hot"], 1)

            def add_strip(strip, buf, uses):
                dve.wait_ge(applied[buf], uses)
                cols = bass.ds(strip * STRIP, STRIP)
                bank = ps_feat if buf else ps_node
                v.tensor_tensor(agg[:, cols], agg[:, cols], bank[:, 0:STRIP], ALU.add).then_inc(strip_added[buf], 1)
                dve.drain()

            def shared(n):
                e = shared_passes[n]
                start_pass(e)
                first = dve.value_load(turns_i[0:1, n, 0:1], min_val=0, max_val=TURNS - 1)
                turns = dve.value_load(turns_i[0:1, n, 1:2], min_val=1, max_val=TURNS)
                dve.wait_ge(own_stored, 16 * (n + 1))

                def turn_beside(strip):
                    with dve.If(turns > strip):
                        edge_turn(e, strip, first)
                        dve.drain()

                if n == 0:
                    dve.sem_inc(strip_added[0], 1)
                    dve.sem_inc(strip_added[1], 1)

                    def segment(strip, seg, windows):
                        if strip:
                            k = windows[0][2]
                            run0 = [i for i, n in enumerate(VISITS[strip * SW:]) if n == k][0] + strip * SW
                            now = visit_now[:, 0:SEG * k]
                            at = visits_upto(strip * SW) + (seg * (SEG * k)) + (
                                visits_upto(run0) - visits_upto(strip * SW) - (run0 - strip * SW) * k)
                            dve.drain()
                            v.tensor_copy(now, visit[:, bass.ds(at, SEG * k)])
                            dve.drain()
                        else:
                            now = visit[:, visits_upto(seg * SEG):visits_upto(seg * SEG + SEG)]
                        if strip == 0:
                            done = 0
                            for k, upto in enumerate(BESIDE_FIRST[seg]):
                                w0 = seg * SEG
                                one_hots(now[:, sum(VISITS[w0:w0 + done]):], windows[done:upto])
                                turn_beside(turn_of(seg, k))
                                done = upto
                        else:
                            one_hots(now, windows)
                        if strip:
                            turn_beside(seg + ((strip - 1) * SEGS + TURNS_FIRST))

                    def strip_ends(strip):
                        if strip:
                            add_strip(strip - 1, 1 - strip % 2, (strip + 1) // 2)

                    each_segment(dve, segment, lambda strip: None, strip_ends)
                    add_strip(STRIPS - 1, 1, STRIPS // 2)
                else:
                    def pair(u, turn0, pace):
                        for seg in range(SEGS):
                            k = SEG * SECOND_VISITS
                            dve.drain()
                            v.tensor_copy(visit_now[:, 0:k], visit[:, bass.ds(u * (SEGS * k) + (visits_upto(NW) + seg * k), k)])
                            dve.drain()
                            one_hots(visit_now, [second_window(u, seg, j) for j in range(SEG)])
                            if seg % 2:
                                turn_beside(turn0 + seg // 2)
                        add_strip(u, 1, u + (STRIPS // 2 + 1))
                        if pace > 2:
                            turn_beside(turn0 + 2)
                        add_strip(u + STRIPS, 0, u + (STRIPS // 2 + 1))

                    each_pair(dve, pair)
                beside = sum(n * pace for n, pace in PACES) if n else (STRIPS - 1) * SEGS + TURNS_FIRST
                with dve.If(turns > beside):
                    with dve.Fori(beside, turns) as i:
                        edge_turn(e, i, first)
                dve.wait_ge(C["evacuated"], NW * (n + 1) + BANKS)
                dve.drain()

            def full(n):
                e = full_passes[n]
                start_pass(e)
                unmask(rows_flat[:, 0:NT])
                dve.wait_ge(own_stored, 16 * (n + 1))
                dve.sem_inc(full_ready[n], 1)
                dve.wait_ge(own_restored[n], 16)
                with dve.Fori(0, TURNS) as i:
                    edge_turn(e, i, 0)
                dve.drain()

            def unmask(shift):
                v.tensor_scalar(shift, dst_rel[:], MASKED / 2, -MASKED, ALU.is_lt, ALU.mult)
                dve.drain()
                v.tensor_tensor(dst_rel[:], dst_rel[:], shift, ALU.add)
                dve.drain()

            def mask_again():
                dve.wait_ge(C["stored_a"], 8 * STRIPS)
                before = region_a[:, 0:NT]
                unmask(before)
                v.tensor_tensor(before.rearrange("p (c t) -> p c t", t=TC), dst_rel[:].rearrange("p (c t) -> p c t", t=TC),
                                chunk_base[:].unsqueeze(2).to_broadcast([P, NCH, TC]), ALU.add)
                dve.drain()
                v.tensor_scalar(before, before, float(IN_COUNTS[1] * STRIP), MASKED, ALU.is_lt, ALU.mult)
                dve.drain()
                v.tensor_tensor(dst_rel[:], dst_rel[:], before, ALU.add)
                dve.drain()

            def verdict(n):
                link(v.tensor_reduce(found[:, 0:1], row_sums[:, 0:IN_COUNTS[n] * SW], AX.X, ALU.max))
                link(v.tensor_reduce(found[:, 1:2], row_sums[:, 0:IN_COUNTS[n] * SW], AX.X, ALU.add))
                link(v.tensor_reduce(found[:, 2:3], count[:, 0:IN_COUNTS[n] * STRIP // P], AX.X, ALU.add))
                link(v.tensor_tensor(found[:, 3:4], found[:, 1:2], found[:, 2:3], ALU.subtract))
                dve.sem_inc(most_ready, 1)
                dve.wait_ge(most_turned, 2 * (n + 1))
                link(v.tensor_reduce(judged[:, 0:1], ps_turn[0:1, 0:P], AX.X, ALU.max))
                link(v.tensor_scalar(judged[:, 0:1], judged[:, 0:1], EXACT, None, ALU.is_gt))
                link(v.tensor_scalar(judged[:, 1:2], ps_extra[0:1, 0:1], 0.0, None, ALU.not_equal))
                link(v.tensor_reduce(judged[:, 2:3], chunk_window[:, 1], AX.X, ALU.max))
                link(v.tensor_reduce(judged[:, 3:4], judged[:, 0:3], AX.X, ALU.max))
                link(v.tensor_scalar(flag[:, n:n + 1], judged[:, 3:4], 0.0, None, ALU.is_gt))
                dve.sem_inc(flag_ready, 1)
                flagged = dve.value_load(flag[0:1, n:n + 1], min_val=0, max_val=1)
                with dve.If(flagged > 0):
                    full(n)
                return flagged

            node_phase(0)
            dve.wait_ge(visits_gathered, 16 * VB)
            block_i = part_columns.rearrange("p (v e) -> p v e", v=VB)
            link(v.tensor_single_scalar(block_i, visit_edges[:, :, 0], P - 1, ALU.bitwise_and))
            link(v.tensor_copy(split_edges[:, :, 0], block_i))
            link(v.tensor_single_scalar(block_i, visit_edges[:, :, 0], 7, ALU.arith_shift_right))
            link(v.tensor_copy(split_edges[:, :, 1], block_i))
            link(v.scalar_tensor_tensor(out=split_edges[:, :, 1], in0=visit_edges[:, :, 1], scalar=float(SB),
                                        in1=split_edges[:, :, 1], op0=ALU.mult, op1=ALU.add))
            link(v.tensor_tensor(split_edges[:, :, 1], split_edges[:, :, 1],
                                 visit_key.unsqueeze(2).to_broadcast([P, VB, P]), ALU.add))
            dve.sem_inc(visits_split, 1)
            for b in range(VB):
                dve.wait_ge(visits_turned, b + 1)
                last = v.tensor_copy(visit[:, b * P:(b + 1) * P].rearrange("p v k -> p k v"),
                                     ps_sum[b % 2][:, 0:2 * P].rearrange("p (k v) -> p k v", k=2))
                last.then_inc(visits_copied, 1)
            dve.wait_ge(visits_copied, VB)
            dve.sem_inc(tables_ready, 1)
            shared(0)
            flagged = verdict(0)
            node_phase(1)
            mask_again()
            with dve.If(flagged < 1):
                shared(1)
            verdict(1)
            dve.drain()
            dve.sem_inc(dense_done, 2)
            dve.wait_ge(x_loaded, 16)
            node_phase(2)
            start_pass(msg_pass)
            unmask(agg[:, 0:NT])
            link(v.memset(agg[:], 0.0))
            with dve.Fori(0, TURNS) as i:
                edge_turn(msg_pass, i, 0)
            dve.wait_ge(msg_pass["added"], NCH + SLOTS)

            dve.sem_inc(fin["free"], 1)
            nodes = ps_node[:].rearrange("p (b d) -> p b d", b=GB)
            sums = ps_feat[:].rearrange("p (b d) -> p b d", b=GB)
            with dve.Fori(0, NG) as g:
                dve.wait_ge(fin["multiplied"], g + 2)
                v.tensor_tensor(tab[:], sums, inv_count[:, bass.ds(g * GB, GB)].unsqueeze(2).to_broadcast([P, GB, D]),
                                ALU.mult).then_inc(fin["steps"], 1)
                dve.wait_ge(fin["steps"], g * 3 + 1)
                v.tensor_tensor(tab[:], nodes, tab[:], ALU.add).then_inc(fin["steps"], 1)
                dve.wait_ge(fin["steps"], g * 3 + 2)
                dve.sem_inc(fin["free"], 1)
                v.tensor_tensor(tab[:], tab[:], upd_b[:, None, :].to_broadcast([P, GB, D]), ALU.add).then_inc(fin["steps"], 1)
                dve.wait_ge(fin["steps"], g * 3 + 3)
                dve.wait_ge(fin["out_free"], g + 1)
                v.scalar_tensor_tensor(out=normed[:], in0=tab[:], scalar=0.0, in1=x1[:, bass.ds(g * GB, GB)],
                                       op0=ALU.max, op1=ALU.add).then_inc(fin["out"], 1)
                dve.wait_ge(fin["out"], g + 1)


def kernel(**inputs):
    import numpy as np
    import concourse.bacc as bacc
    from concourse.bass_utils import run_bass_kernel_spmd

    nc = bacc.Bacc("TRN2", target_bir_lowering=False, num_devices=1)
    x = np.zeros((NP, D), np.float32)
    x[:N] = inputs["x"]
    src = np.zeros(EP, np.int32)
    src[:E] = inputs["src"]
    dst = np.full(EP, N, np.int32)
    dst[:E] = inputs["dst"]
    attr = np.zeros((EP, DE), np.float32)
    attr[:E] = inputs["edge_attr_32"]
    long_src = np.concatenate([src, np.zeros(EDGE_ROWS * ROW + P - EP, np.int32)])
    long_dst = np.concatenate([dst, np.full(EDGE_ROWS * ROW + P - EP, N, np.int32)])
    at = ROW * np.arange(EDGE_ROWS)[:, None] + np.arange(P)[None, :]
    visit_of = np.zeros((3, VB * P), np.int32)
    visit_of[0, :sum(VISITS)] = np.repeat(np.arange(2 * NW) * W, VISITS)
    visit_of[1, :sum(VISITS)] = np.concatenate([np.arange(k) for k in VISITS]) * (P // ROW)
    visit_of[2, :sum(VISITS)] = np.repeat(-np.arange(2 * NW) * KEYS, VISITS)
    visit_of = visit_of.reshape(3, VB, P).transpose(2, 0, 1)
    node_half = P * np.arange(SB)[None, :] + np.arange(P)[:, None] - 0.5
    constants = np.concatenate([np.eye(P), np.tile(np.arange(P), (P, 1)), np.tile(np.arange(KEYS), (P, 1)),
                                np.triu(np.ones((P, P)), 1), visit_of[:, 2], node_half, -node_half], 1).astype(np.float32)
    arrays = {
        "x_nodes": x.reshape(NB, P, D).transpose(1, 0, 2),
        "src_t": np.concatenate([src, np.zeros(SLOTS * CE, np.int32)]).reshape(-1, P).T,
        "dst_t": dst.reshape(NT, P).T,
        "dst_rows": dst.reshape(CR, CQ, CE),
        "attr_t": attr.reshape(NCH, TC, P, DE).transpose(1, 3, 0, 2).reshape(P, NCH, P),
        "consts": constants,
        "visit_plan": visit_of[:, :2],
        "edge_rows": np.concatenate([long_src[at], long_dst[at]], 1),
    }
    for name in ("L0_gnn_W1", "L0_gnn_b1", "L0_gnn_W2", "L0_gnn_b2", "L1_gnn_W1", "L1_gnn_b1", "L1_gnn_W2", "L1_gnn_b2"):
        arrays[name] = inputs[name]
    arrays = {f"{k}_in": np.ascontiguousarray(a) for k, a in arrays.items()}
    t = {k[:-3]: nc.dram_tensor(k, a.shape, mybir.dt.from_np(a.dtype), kind="ExternalInput").ap() for k, a in arrays.items()}
    out = nc.dram_tensor("out_nodes", (NP, D), F32, kind="ExternalOutput").ap()
    build(nc, t, out)
    r = run_bass_kernel_spmd(nc, [arrays], core_ids=[0])
    return r.results[0]["out_nodes"][:N]
```
